# Optimizing a Trainium2 kernel written in Bass

```python
import numpy as np
import jax
import jax.numpy as jnp

def _softmax(x, axis=-1):
    return jax.nn.softmax(x, axis=axis)

def _gelu(x):
    return jax.nn.gelu(x, approximate=True)

def _silu(x):
    return jax.nn.silu(x)

def _sigmoid(x):
    return jax.nn.sigmoid(x)

def _layernorm(x, axis=-1, eps=1e-05):
    m = jnp.mean(x, axis=axis, keepdims=True)
    v = jnp.var(x, axis=axis, keepdims=True)
    return (x - m) / jnp.sqrt(v + eps)

def _scatter_add(tgt, idx, src, axis=0):
    return tgt.at[idx].add(src)

def _segment_sum(src, seg, n):
    return jax.ops.segment_sum(src, seg, n)
kernel_name = 'mk_metaformer_d1_conv_nhwc512_r2_6e2c9d'

def setup_inputs(seed: int=0):
    np.random.seed(seed)
    _w = jnp.asarray

    def _rec_inputs():
        import jax
        import jax.numpy as jnp
        _gk = jax.random.key(seed)
        x = 1.648e-05 + 1 * jax.random.normal(jax.random.fold_in(_gk, 1), (8, 48, 48, 256), jnp.float32)
        return x
    x = _rec_inputs()

    def _L0_conv_setup():
        import jax, jax.numpy as jnp
        import numpy as np
        D_MODEL = 256
        D_STATE = 16
        EXPAND = 2
        DT_RANK = 8
        D_INNER = EXPAND * D_MODEL
        LN_EPS = 1e-05

        def _ss2d(x, W_in, conv_k, W_xproj, W_dt, b_dt, A_log, Dskip, W_dtN, b_dtN, ln_g, ln_b, W_out, b_out):
            B, H, W_, _ = x.shape
            L = H * W_
            xz = x @ W_in
            xh, z = jnp.split(xz, 2, axis=-1)
            xc = jax.lax.conv_general_dilated(xh, conv_k, window_strides=(1, 1), padding='SAME', dimension_numbers=('NHWC', 'HWIO', 'NHWC'), feature_group_count=D_INNER)
            xp = xc @ W_xproj
            dt_r = xp[..., :DT_RANK]
            Bp = xp[..., DT_RANK:DT_RANK + D_STATE]
            Cp = xp[..., DT_RANK + D_STATE:]
            dt = dt_r @ W_dt + b_dt
            x_seq = xc.reshape(B, L, D_INNER)
            dt_seq = jax.nn.softplus(dt.reshape(B, L, D_INNER))
            B_seq = Bp.reshape(B, L, D_STATE)
            C_seq = Cp.reshape(B, L, D_STATE)
            A = -jnp.exp(A_log)
            dtN = dt_seq @ W_dtN + b_dtN

            def step(h, t):
                x_t, dt_t, dtN_t, B_t, C_t = t
                dA = jnp.exp(dt_t[:, :, None] * A)
                dB = dtN_t * B_t
                h = dA * h + dB[:, None, :] * x_t[:, :, None]
                y = jnp.einsum('bdn,bn->bd', h, C_t) + Dskip * x_t
                return (h, y)
            h0 = jnp.zeros((B, D_INNER, D_STATE), x.dtype)
            xs = (x_seq.transpose(1, 0, 2), dt_seq.transpose(1, 0, 2), dtN.transpose(1, 0, 2), B_seq.transpose(1, 0, 2), C_seq.transpose(1, 0, 2))
            _, ys = jax.lax.scan(step, h0, xs)
            y = ys.transpose(1, 0, 2).reshape(B, H, W_, D_INNER)
            mu = y.mean(-1, keepdims=True)
            var = ((y - mu) ** 2).mean(-1, keepdims=True)
            y = (y - mu) / jnp.sqrt(var + LN_EPS) * ln_g + ln_b
            y = y * jax.nn.silu(z)
            return y @ W_out + b_out
        key = jax.random.key(seed)
        ks = jax.random.split(key, 10)
        B, H, W = (8, 48, 48)
        inp = {'x': jax.random.normal(ks[0], (B, H, W, D_MODEL), jnp.float32), 'W_in': jax.random.normal(ks[1], (D_MODEL, 2 * D_INNER), jnp.float32) * 0.02, 'conv_k': jax.random.normal(ks[2], (3, 3, 1, D_INNER), jnp.float32) * 0.1, 'W_xproj': jax.random.normal(ks[3], (D_INNER, DT_RANK + 2 * D_STATE), jnp.float32) * 0.02, 'W_dt': jax.random.uniform(ks[4], (DT_RANK, D_INNER), jnp.float32, -0.1, 0.1), 'b_dt': jnp.full((D_INNER,), 0.1, jnp.float32), 'A_log': jax.random.normal(ks[5], (D_STATE,), jnp.float32) * 0.02, 'Dskip': jnp.ones((D_INNER,), jnp.float32), 'W_dtN': jax.random.normal(ks[6], (D_INNER, D_STATE), jnp.float32) * 0.02, 'b_dtN': jnp.zeros((D_STATE,), jnp.float32), 'ln_g': jnp.ones((D_INNER,), jnp.float32), 'ln_b': jnp.zeros((D_INNER,), jnp.float32), 'W_out': jax.random.normal(ks[7], (D_INNER, D_MODEL), jnp.float32) * 0.02, 'b_out': jnp.zeros((D_MODEL,), jnp.float32)}
        return inp
    _L0_conv_all = _L0_conv_setup()
    _L0_conv_in = {k: v for k, v in _L0_conv_all.items() if k in ('W_in', 'conv_k', 'W_xproj', 'W_dt', 'b_dt', 'A_log', 'Dskip', 'W_dtN', 'b_dtN', 'ln_g', 'ln_b', 'W_out', 'b_out')}
    del _L0_conv_all

    def _L0_ffn_setup():
        import jax, jax.numpy as jnp
        import numpy as np
        MARK_AX = 0
        OPCODE_BASE = 16
        OP_SHL = OPCODE_BASE + 23
        OP_SHR = OPCODE_BASE + 24
        ALU_LO = 32
        ALU_HI = 40
        AX_CARRY_LO = 48
        OUTPUT_LO = 64
        OUTPUT_HI = 72
        B, SEQ, D = (8, 16384, 256)
        key = jax.random.key(seed)
        ks = jax.random.split(key, 6)
        x = jax.random.uniform(ks[0], (B, SEQ, D), dtype=jnp.float32) * 0.4
        mark = (jax.random.uniform(ks[1], (B, SEQ)) < 0.75).astype(jnp.float32)
        op_sel = jax.random.randint(ks[2], (B, SEQ), 0, 3)
        lo = jax.random.randint(ks[3], (B, SEQ), 0, 16)
        hi = jax.random.randint(ks[4], (B, SEQ), 0, 16)
        sa = jax.random.randint(ks[5], (B, SEQ), 0, 16)
        oh = lambda idx: jax.nn.one_hot(idx, 16, dtype=jnp.float32)
        x = x.at[..., MARK_AX].set(mark)
        x = x.at[..., OP_SHL].set((op_sel == 1).astype(jnp.float32))
        x = x.at[..., OP_SHR].set((op_sel == 2).astype(jnp.float32))
        x = x.at[..., ALU_LO:ALU_LO + 16].set(oh(lo))
        x = x.at[..., ALU_HI:ALU_HI + 16].set(oh(hi))
        x = x.at[..., AX_CARRY_LO:AX_CARRY_LO + 16].set(oh(sa))
        return {'x_bd': x}
    _L0_ffn_all = _L0_ffn_setup()
    _L0_ffn_in = {k: v for k, v in _L0_ffn_all.items() if k in ()}
    del _L0_ffn_all
    return {'x': x, 'L0_conv_W_in': _L0_conv_in['W_in'], 'L0_conv_conv_k': _L0_conv_in['conv_k'], 'L0_conv_W_xproj': _L0_conv_in['W_xproj'], 'L0_conv_W_dt': _L0_conv_in['W_dt'], 'L0_conv_b_dt': _L0_conv_in['b_dt'], 'L0_conv_A_log': _L0_conv_in['A_log'], 'L0_conv_Dskip': _L0_conv_in['Dskip'], 'L0_conv_W_dtN': _L0_conv_in['W_dtN'], 'L0_conv_b_dtN': _L0_conv_in['b_dtN'], 'L0_conv_ln_g': _L0_conv_in['ln_g'], 'L0_conv_ln_b': _L0_conv_in['ln_b'], 'L0_conv_W_out': _L0_conv_in['W_out'], 'L0_conv_b_out': _L0_conv_in['b_out']}

def reference(x, L0_conv_W_in, L0_conv_conv_k, L0_conv_W_xproj, L0_conv_W_dt, L0_conv_b_dt, L0_conv_A_log, L0_conv_Dskip, L0_conv_W_dtN, L0_conv_b_dtN, L0_conv_ln_g, L0_conv_ln_b, L0_conv_W_out, L0_conv_b_out):
    import jax
    import jax.numpy as jnp

    def _L0_conv_ref(x, W_in, conv_k, W_xproj, W_dt, b_dt, A_log, Dskip, W_dtN, b_dtN, ln_g, ln_b, W_out, b_out):
        import jax, jax.numpy as jnp
        import numpy as np
        D_MODEL = 256
        D_STATE = 16
        EXPAND = 2
        DT_RANK = 8
        D_INNER = EXPAND * D_MODEL
        LN_EPS = 1e-05

        def _ss2d(x, W_in, conv_k, W_xproj, W_dt, b_dt, A_log, Dskip, W_dtN, b_dtN, ln_g, ln_b, W_out, b_out):
            B, H, W_, _ = x.shape
            L = H * W_
            xz = x @ W_in
            xh, z = jnp.split(xz, 2, axis=-1)
            xc = jax.lax.conv_general_dilated(xh, conv_k, window_strides=(1, 1), padding='SAME', dimension_numbers=('NHWC', 'HWIO', 'NHWC'), feature_group_count=D_INNER)
            xp = xc @ W_xproj
            dt_r = xp[..., :DT_RANK]
            Bp = xp[..., DT_RANK:DT_RANK + D_STATE]
            Cp = xp[..., DT_RANK + D_STATE:]
            dt = dt_r @ W_dt + b_dt
            x_seq = xc.reshape(B, L, D_INNER)
            dt_seq = jax.nn.softplus(dt.reshape(B, L, D_INNER))
            B_seq = Bp.reshape(B, L, D_STATE)
            C_seq = Cp.reshape(B, L, D_STATE)
            A = -jnp.exp(A_log)
            dtN = dt_seq @ W_dtN + b_dtN

            def step(h, t):
                x_t, dt_t, dtN_t, B_t, C_t = t
                dA = jnp.exp(dt_t[:, :, None] * A)
                dB = dtN_t * B_t
                h = dA * h + dB[:, None, :] * x_t[:, :, None]
                y = jnp.einsum('bdn,bn->bd', h, C_t) + Dskip * x_t
                return (h, y)
            h0 = jnp.zeros((B, D_INNER, D_STATE), x.dtype)
            xs = (x_seq.transpose(1, 0, 2), dt_seq.transpose(1, 0, 2), dtN.transpose(1, 0, 2), B_seq.transpose(1, 0, 2), C_seq.transpose(1, 0, 2))
            _, ys = jax.lax.scan(step, h0, xs)
            y = ys.transpose(1, 0, 2).reshape(B, H, W_, D_INNER)
            mu = y.mean(-1, keepdims=True)
            var = ((y - mu) ** 2).mean(-1, keepdims=True)
            y = (y - mu) / jnp.sqrt(var + LN_EPS) * ln_g + ln_b
            y = y * jax.nn.silu(z)
            return y @ W_out + b_out
        return _ss2d(x, W_in, conv_k, W_xproj, W_dt, b_dt, A_log, Dskip, W_dtN, b_dtN, ln_g, ln_b, W_out, b_out)

    def _L0_ffn_ref(x_bd):
        import jax, jax.numpy as jnp
        import numpy as np
        MARK_AX = 0
        OPCODE_BASE = 16
        OP_SHL = OPCODE_BASE + 23
        OP_SHR = OPCODE_BASE + 24
        ALU_LO = 32
        ALU_HI = 40
        AX_CARRY_LO = 48
        OUTPUT_LO = 64
        OUTPUT_HI = 72
        B, SEQ, D = (8, 16384, 256)
        hot = x_bd > 0.5
        first16 = lambda off: jnp.argmax(hot[..., off:off + 16], axis=-1).astype(jnp.int32)
        lo = first16(ALU_LO)
        hi = first16(ALU_HI)
        sa = first16(AX_CARRY_LO)
        val = lo + 16 * hi
        shl = jnp.left_shift(val, sa) & 255
        shr = jnp.right_shift(val, sa)
        mark = hot[..., MARK_AX]
        is_shl = hot[..., OP_SHL]
        is_shr = jnp.logical_and(hot[..., OP_SHR], jnp.logical_not(is_shl))
        act_shl = jnp.logical_and(mark, is_shl)
        act_shr = jnp.logical_and(mark, is_shr)
        active = jnp.logical_or(act_shl, act_shr)
        res = jnp.where(act_shl, shl, jnp.where(act_shr, shr, 0))
        res = jnp.clip(res, 0, 255)
        rlo = res & 15
        rhi = res >> 4
        amp = 2.0 * active.astype(x_bd.dtype)
        add_lo = amp[..., None] * jax.nn.one_hot(rlo, 16, dtype=x_bd.dtype)
        add_hi = amp[..., None] * jax.nn.one_hot(rhi, 16, dtype=x_bd.dtype)
        out = x_bd.at[..., OUTPUT_LO:OUTPUT_LO + 16].add(add_lo)
        out = out.at[..., OUTPUT_HI:OUTPUT_HI + 16].add(add_hi)
        return out

    def _gn(v, G=32, eps=1e-05):
        B_, H_, W_, C_ = v.shape
        g = v.reshape(B_, H_, W_, G, C_ // G)
        m = jnp.mean(g, axis=(1, 2, 4), keepdims=True)
        s = jnp.var(g, axis=(1, 2, 4), keepdims=True)
        return ((g - m) / jnp.sqrt(s + eps)).reshape(v.shape)

    def _ln_c(v, eps=1e-06):
        m = jnp.mean(v, axis=-1, keepdims=True)
        s = jnp.var(v, axis=-1, keepdims=True)
        return (v - m) / jnp.sqrt(s + eps)

    def _ln_t(v, eps=1e-05):
        m = jnp.mean(v, axis=-1, keepdims=True)
        s = jnp.var(v, axis=-1, keepdims=True)
        return (v - m) / jnp.sqrt(s + eps)

    def _to_tokens(v):
        B_, H_, W_, C_ = v.shape
        return v.reshape(B_, H_ * W_, C_)

    def _from_tokens(t, like):
        return t.reshape(like.shape)
    x = x + _L0_conv_ref(_ln_c(x), L0_conv_W_in, L0_conv_conv_k, L0_conv_W_xproj, L0_conv_W_dt, L0_conv_b_dt, L0_conv_A_log, L0_conv_Dskip, L0_conv_W_dtN, L0_conv_b_dtN, L0_conv_ln_g, L0_conv_ln_b, L0_conv_W_out, L0_conv_b_out)
    t = _to_tokens(x)
    t = t + _L0_ffn_ref(_ln_t(t))
    x = _from_tokens(t, x)
    return x

_drawn_inputs = setup_inputs


def setup_inputs(seed=0):
    import zlib

    import numpy as np

    out = dict(_drawn_inputs(seed))
    spreads = {'L0_conv_b_dt': (0.10000000149011612, 0.6),
     'L0_conv_Dskip': (1.0, 0.6),
     'L0_conv_b_dtN': (0.0, 0.8),
     'L0_conv_ln_g': (1.0, 0.6),
     'L0_conv_ln_b': (0.0, 0.8),
     'L0_conv_b_out': (0.0, 0.1)}
    factors = {'L0_conv_W_xproj': 8.0, 'L0_conv_W_dt': 8.0, 'L0_conv_A_log': 33.295, 'L0_conv_W_dtN': 8.0}
    for name, (base, spread) in spreads.items():
        noise = np.random.default_rng([zlib.crc32(name.encode()), seed]).standard_normal(out[name].shape)
        drawn = base * np.exp(spread * noise) if base else spread * noise
        out[name] = jnp.asarray(drawn.astype(out[name].dtype))
    for name, factor in factors.items():
        out[name] = (out[name] * factor).astype(out[name].dtype)
    return out
```

```python
from contextlib import ExitStack

import concourse.bass as bass
from concourse import mybir

F32 = mybir.dt.float32
I32 = mybir.dt.int32
ALU = mybir.AluOpType
ACT = mybir.ActivationFunctionType
AX_X = mybir.AxisListType.X

P = 128
IMAGES, SIDE, DM = 8, 48, 256
DI, NS, DTR = 512, 16, 8
NC = DI // P
KM = DM // P
ROWS = 8
TOK = ROWS * SIDE
KT = TOK // P
TPB = SIDE // ROWS
TILES = IMAGES * TPB
QS = 4
NG = 4
STEPS = NG * QS
RING = 4
XH_TILES = 3
XLN_TILES = 3
DT_CLAMP = 40.0
SEM_DMA = 16
B_ROW, C_ROW = 32, 64
XP_ROWS = 96


class Tile:

    def __init__(self, b, s):
        self.b, self.s = b, s
        self.idx = b * TPB + s
        self.half = b * (TPB // 2) + s // 2

    def at(self, n):
        return Tile(self.b, self.s + n)

    def exists(self):
        return not isinstance(self.b, int) or 0 <= self.idx < TILES

    def after(self, n):
        return not isinstance(self.b, int) or self.idx >= n

    def first_of_image(self):
        return self.s % TPB == 0

    def last_of_image(self):
        return self.s % TPB == TPB - 1


def conv_parts(t):
    slot = t.s % XH_TILES
    ring_rows = XH_TILES * ROWS
    parts = []
    for dy in (0, -1, 1):
        for dx in (0, -1, 1):
            tap = 3 * (dy + 1) + dx + 1
            o0, n = 0, ROWS
            if dy == -1 and t.first_of_image():
                o0, n = 1, ROWS - 1
            if dy == 1 and t.last_of_image():
                n = ROWS - 1
            r0 = slot * ROWS + o0 + dy
            if r0 < 0:
                parts.append((tap, dx, ring_rows - 1, 0, 1))
                parts.append((tap, dx, 0, 1, n - 1))
            elif r0 + n > ring_rows:
                parts.append((tap, dx, r0, o0, n - 1))
                parts.append((tap, dx, 0, o0 + n - 1, 1))
            else:
                parts.append((tap, dx, r0, o0, n))
    return parts


def build(nc, x, W_in, conv_k, W_xproj, W_dt, b_dt, A_log, Dskip, W_dtN, b_dtN, ln_g, ln_b, W_out, b_out, out):
    x_tiles = x.rearrange("b (s r) w m -> (b s) (r w) m", r=ROWS).rearrange("i (k p) m -> i p k m", p=P)
    out_tiles = out.rearrange("b (s r) w m -> (b s) (r w) m", r=ROWS).rearrange("i (k p) m -> i p k m", p=P)

    with ExitStack() as ctx:
        def sb(name, shape, dt=F32):
            return ctx.enter_context(nc.sbuf_tensor(name, shape, dt))

        def pb(name):
            return ctx.enter_context(nc.psum_tensor(name, [P, 512], F32))

        def sem(name):
            return ctx.enter_context(nc.semaphore(name))

        win = sb("win", [P, KM, 2 * DI])
        wout = sb("wout", [P, NG, DM])
        wxp = sb("wxp", [P, NC, XP_ROWS])
        wdt = sb("wdt", [DTR, DI])
        wdtn = sb("wdtn", [P, NC, B_ROW + NS])
        taps = sb("taps", [P, NC, 9])
        conv_w = sb("conv_w", [P, NC, 9, P])
        ident = sb("ident", [P, P])
        mean_w = sb("mean_w", [P, P])
        nsum = sb("nsum", [P, 32])
        skip_w = sb("skip_w", [P, NG, NC, 32])
        dskip4 = sb("dskip4", [P, NG, NC])
        bdt = sb("bdt", [P, NC])
        bdtn = sb("bdtn", [P, 1])
        gam = sb("gam", [P, NG])
        bet = sb("bet", [P, NG])
        a4 = sb("a4", [P, QS])
        bout = sb("bout", [1, DM])
        ones_row = sb("ones_row", [1, P])
        one_c = sb("one_c", [P, 1])
        eps1 = sb("eps1", [P, 1])
        eps2 = sb("eps2", [P, 1])
        one_nc = sb("one_nc", [P, NC])
        idx16 = sb("idx16", [P, 16])
        score16 = sb("score16", [P, 16])
        xin = sb("xin", [P, KT, DM])
        st1 = sb("st1", [P, KT, 6])
        wait_pad1 = sb("wait_pad1", [P, 1])
        wait_pad2 = sb("wait_pad2", [P, 1])
        mv1 = sb("mv1", [P, KT, 2])
        rs1 = sb("rs1", [P, KT])
        xlnT = sb("xlnT", [P, XLN_TILES, KM, TOK])
        xh = sb("xh", [P, NC, XH_TILES * ROWS, SIDE + 2])
        xc = sb("xc", [P, 2, NC, TOK])
        xp = sb("xp", [XP_ROWS, TOK])
        dbt = sb("dbt", [B_ROW + NS, TOK])
        spt = sb("spt", [P, 2, TOK])
        dt = sb("dt", [P, NC, TOK])
        dt4 = sb("dt4", [P, 2, NC, TOK])
        x4 = sb("x4", [P, 2, NC, TOK])
        db4 = sb("db4", [P, 2, QS, TOK])
        c4 = sb("c4", [P, 2, QS, TOK])
        a = sb("a", [P, 2, NC, TOK])
        uhg = sb("uhg", [P, RING, NC, TOK])
        carry = sb("carry", [P, STEPS, NC])
        y = sb("y", [P, 2, NG, TOK])
        sq = sb("sq", [P, 2, TOK])
        rstd = sb("rstd", [P, TOK])
        sz = sb("sz", [P, NG, TOK])
        res = sb("res", [P, KT, DM])
        st2 = sb("st2", [P, KT, 6])
        mv2 = sb("mv2", [P, KT, 2])
        rs2 = sb("rs2", [P, KT])
        sc1 = sb("sc1", [P, KT])
        sc2 = sb("sc2", [P, KT])
        hot = sb("hot", [P, KT, 64])
        score = sb("score", [P, KT, 3, 16])
        best = sb("best", [P, KT, 3])
        found = sb("found", [P, KT, 3])
        nib = sb("nib", [P, KT, 3], I32)
        val = sb("val", [P, KT], I32)
        shl = sb("shl", [P, KT], I32)
        shr = sb("shr", [P, KT], I32)
        dif = sb("dif", [P, KT])
        resi = sb("resi", [P, KT], I32)
        rnib = sb("rnib", [P, KT, 2], I32)
        amp = sb("amp", [P, KT])
        hots = sb("hots", [P, KT, 2, 16])

        ps_y = [pb(f"ps_y{n}") for n in range(2)]
        ps_c = [pb(f"ps_c{n}") for n in range(2)]
        ps_d = [pb(f"ps_d{n}") for n in range(2)]
        ps_w = [pb(f"ps_w{n}") for n in range(2)]

        bounce = nc.dram_tensor("bounce", [2, 2, NS, TOK], F32, kind="Internal").ap()

        weights_in = sem("weights_in")
        pads_set = sem("pads_set")
        masks_set = sem("masks_set")
        zeros_set = sem("zeros_set")
        ident_set = sem("ident_set")
        nsum_set = sem("nsum_set")
        idx_set = sem("idx_set")
        a_exp = sem("a_exp")
        consts_set = sem("consts_set")
        xin_loaded = sem("xin_loaded")
        ln1_stat = sem("ln1_stat")
        ln1_var = sem("ln1_var")
        ln1_log = sem("ln1_log")
        ln1_rstd = sem("ln1_rstd")
        xln_ready = sem("xln_ready")
        xt_done = sem("xt_done")
        xlnT_ready = sem("xlnT_ready")
        proj_done = sem("proj_done")
        xh_ready = sem("xh_ready")
        conv_done = sem("conv_done")
        xc_ready = sem("xc_ready")
        xproj_done = sem("xproj_done")
        xp_ready = sem("xp_ready")
        dtp_done = sem("dtp_done")
        clamped = sem("clamped")
        sp_exp = sem("sp_exp")
        sp_log = sem("sp_log")
        dt_ready = sem("dt_ready")
        dtn_done = sem("dtn_done")
        db_ready = sem("db_ready")
        bounced = sem("bounced")
        dt4_loaded = [sem(f"dt4_loaded{n}") for n in range(2)]
        x4_loaded = [sem(f"x4_loaded{n}") for n in range(2)]
        db4_loaded = [sem(f"db4_loaded{n}") for n in range(2)]
        c4_loaded = [sem(f"c4_loaded{n}") for n in range(2)]
        a_ready = sem("a_ready")
        u_ready = sem("u_ready")
        h_ready = sem("h_ready")
        carry_saved = sem("carry_saved")
        g_ready = sem("g_ready")
        g_used = sem("g_used")
        skip_added = sem("skip_added")
        y_ready = sem("y_ready")
        mean_done = sem("mean_done")
        centred = sem("centred")
        squared = sem("squared")
        sq_used = sem("sq_used")
        var_log = sem("var_log")
        rstd_ready = sem("rstd_ready")
        z_done = sem("z_done")
        sz_ready = sem("sz_ready")
        normed = sem("normed")
        gated = sem("gated")
        out_done = sem("out_done")
        res_loaded = sem("res_loaded")
        res_added = sem("res_added")
        ln2_stat = sem("ln2_stat")
        ln2_var = sem("ln2_var")
        ln2_log = sem("ln2_log")
        ln2_rstd = sem("ln2_rstd")
        ffn = sem("ffn")
        marked = sem("marked")
        final_ready = sem("final_ready")
        out_stored = sem("out_stored")

        WEIGHT_DMAS = NC + 3 * NC + 1 + NG * KM + 5 + 4 * (1 + NC) + 3 * NC

        block = ctx.enter_context(nc.Block())

        @block.sync
        def _(sp):
            def load(dst, src):
                sp.dma_start(dst, src, allow_slow_non_contiguous=True).then_inc(weights_in, SEM_DMA)

            sp.wait_ge(zeros_set, 2)
            for c in range(NC):
                load(taps[:, c, :], conv_k[:, :, 0, c * P:(c + 1) * P].rearrange("a b p -> p (a b)"))
            for c in range(NC):
                rows = slice(c * P, (c + 1) * P)
                load(wxp[:, c, 0:DTR], W_xproj[rows, 0:DTR])
                load(wxp[:, c, B_ROW:B_ROW + NS], W_xproj[rows, DTR:DTR + NS])
                load(wxp[:, c, C_ROW:C_ROW + NS], W_xproj[rows, DTR + NS:DTR + 2 * NS])
            load(win[:, :, 0:DI], W_in.rearrange("(k p) n -> p k n", p=P)[:, :, 0:DI])
            z_cols = W_in.rearrange("(k p) (h c g r) -> p k h g c r", p=P, h=2, c=NC, g=NG)
            for g in range(NG):
                for k in range(KM):
                    lo = DI + g * P
                    load(win[:, k, lo:lo + P].rearrange("p (c r) -> p c r", c=NC), z_cols[:, k, 1, g])
            load(wdt[:], W_dt)
            load(wdtn[:, :, B_ROW:B_ROW + NS], W_dtN.rearrange("(c p) n -> p c n", p=P))
            load(bdt[:], b_dt.rearrange("(c p) -> p c", p=P))
            load(bdtn[B_ROW:B_ROW + NS, :], b_dtN.rearrange("(n o) -> n o", o=1))
            load(bout[:], b_out.rearrange("(o m) -> o m", o=1))
            a_rows = A_log.rearrange("(o q k) -> k o q", o=1, k=4)
            for k in range(4):
                quad = slice(32 * k, 32 * k + 32)
                load(a4[quad, :], a_rows[k].broadcast_to([32, QS]))
                for c in range(NC):
                    load(dskip4[quad, :, c], Dskip[c * P:(c + 1) * P].rearrange("(g p) -> p g", g=NG))
            for c in range(NC):
                part = slice(32 * c, 32 * c + 32)
                mine = slice(c * P, (c + 1) * P)
                load(gam[part, :], ln_g[mine].rearrange("(g p) -> p g", g=NG))
                load(bet[part, :], ln_b[mine].rearrange("(g p) -> p g", g=NG))
                load(wout[part, :, :], W_out[mine, :].rearrange("(g p) m -> p g m", g=NG))

            def load_x(t):
                if t.after(1):
                    sp.wait_ge(xt_done, t.idx * KM)
                sp.dma_start(xin[:], x_tiles[t.idx]).then_inc(xin_loaded, SEM_DMA)

            def load_group(t, g):
                buf = g % 2
                if g == 0:
                    sp.wait_ge(dt_ready, t.idx * NC + NC)
                    sp.wait_ge(xc_ready, t.idx * NC + NC)
                if t.after(1) or g > 1:
                    steps = t.idx * STEPS + QS * (g - 1)
                    sp.wait_ge(a_ready, steps)
                    sp.wait_ge(u_ready, steps)
                    sp.wait_ge(skip_added, steps)
                src = slice(32 * g, 32 * g + 32)
                for k in range(4):
                    quad = slice(32 * k, 32 * k + 32)
                    sp.dma_start(dt4[quad, buf], dt[src]).then_inc(dt4_loaded[buf], SEM_DMA)
                for k in range(4):
                    quad = slice(32 * k, 32 * k + 32)
                    sp.dma_start(x4[quad, buf], xc[src, t.s % 2]).then_inc(x4_loaded[buf], SEM_DMA)

            def load_states(t):
                par = t.s % 2
                sp.wait_ge(db_ready, t.idx + 1)
                sp.wait_ge(xp_ready, t.idx + 1)
                if t.after(2):
                    sp.wait_ge(u_ready, t.at(-1).idx * STEPS)
                    sp.wait_ge(g_ready, t.at(-1).idx * STEPS)
                    full = t.half * (4 * SEM_DMA)
                    sp.wait_ge(db4_loaded[par], full)
                    sp.wait_ge(c4_loaded[par], full)
                sp.dma_start(bounce[par, 0], dbt[B_ROW:B_ROW + NS, :]).then_inc(bounced, SEM_DMA)
                sp.dma_start(bounce[par, 1], xp[C_ROW:C_ROW + NS, :]).then_inc(bounced, SEM_DMA)
                sp.wait_ge(bounced, t.idx * (2 * SEM_DMA) + 2 * SEM_DMA)
                for which, dst, done in ((0, db4, db4_loaded), (1, c4, c4_loaded)):
                    rows = bounce[par, which].rearrange("(q k) t -> k q t", k=4)
                    for k in range(4):
                        quad = slice(32 * k, 32 * k + 32)
                        sp.dma_start(dst[quad, par], rows[k].unsqueeze(0).broadcast_to([32, QS, TOK])) \
                          .then_inc(done[par], SEM_DMA)

            def load_residual(t):
                if t.after(1):
                    sp.wait_ge(out_stored, t.idx * SEM_DMA)
                sp.dma_start(res[:], x_tiles[t.idx]).then_inc(res_loaded, SEM_DMA)

            def store(t):
                sp.wait_ge(final_ready, t.idx + 1)
                sp.dma_start(out_tiles[t.idx], res[:]).then_inc(out_stored, SEM_DMA)

            def body(b):
                for s in range(TPB):
                    i = Tile(b, s)
                    if i.at(3).exists():
                        load_x(i.at(3))
                    load_group(i, 1)
                    load_group(i, 2)
                    load_group(i, 3)
                    if i.at(-2).exists():
                        store(i.at(-2))
                    if i.at(-1).exists():
                        load_residual(i.at(-1))
                    if i.at(1).exists():
                        load_group(i.at(1), 0)
                        load_states(i.at(1))

            for s in range(3):
                load_x(Tile(0, s))
            load_group(Tile(0, 0), 0)
            load_states(Tile(0, 0))
            body(0)
            with sp.Fori(1, IMAGES - 1) as b:
                body(b)
            body(IMAGES - 1)
            store(Tile(IMAGES - 1, TPB - 2))
            load_residual(Tile(IMAGES - 1, TPB - 1))
            store(Tile(IMAGES - 1, TPB - 1))
            sp.wait_ge(out_stored, TILES * SEM_DMA)
            sp.wait_ge(bounced, TILES * 2 * SEM_DMA)

        @block.tensor
        def _(pe):
            def transpose_x(t, ps_free):
                pe.wait_ge(xln_ready, t.idx + 1)
                for m in range(KM):
                    ps_free(m)
                    for k in range(KT):
                        mm = pe.transpose(ps_c[m][:, k * P:(k + 1) * P], xin[:, k, m * P:(m + 1) * P], ident[:])
                    mm.then_inc(xt_done, 1)

            def project(t, c):
                if c == 0:
                    pe.wait_ge(xlnT_ready, t.idx * KM + KM)
                if c >= 2:
                    pe.wait_ge(xh_ready, t.idx * NC + c - 1)
                for m in range(KM):
                    mm = pe.matmul(ps_c[c % 2][:, 0:TOK], win[:, m, c * P:(c + 1) * P], xlnT[:, t.s % XLN_TILES, m, :],
                                   start=m == 0, stop=m == KM - 1)
                mm.then_inc(proj_done, 1)

            def conv(t, lo, hi, newest):
                parts = conv_parts(t)
                for n in range(lo, hi):
                    c, j = n // 9, n % 9
                    tap = parts_of_tap(parts, j)
                    if j == 0:
                        if c < 2:
                            pe.wait_ge(xh_ready, newest.idx * NC + c + 3)
                        else:
                            pe.wait_ge(xc_ready, t.idx * NC + c - 1)
                        if c == 0:
                            pe.wait_ge(xh_ready, newest.idx * NC + NC)
                    for m, (w, dx, r0, o0, rows) in enumerate(tap):
                        mm = pe.matmul(ps_c[c % 2][:, o0 * SIDE:(o0 + rows) * SIDE],
                                       conv_w[:, c, w, :], xh[:, c, r0:r0 + rows, 1 + dx:1 + dx + SIDE],
                                       start=j == 0, stop=j == 8 and m == len(tap) - 1, skip_group_check=True)
                    if j == 8:
                        mm.then_inc(conv_done, 1)

            def parts_of_tap(parts, j):
                order = []
                for part in parts:
                    if part[0] not in order:
                        order.append(part[0])
                return [part for part in parts if part[0] == order[j]]

            def x_project(t):
                pe.wait_ge(xc_ready, t.idx * NC + NC)
                if t.after(1):
                    pe.wait_ge(db_ready, t.idx)
                if t.after(2):
                    pe.wait_ge(centred, t.idx - 1)
                for c in range(NC):
                    mm = pe.matmul(ps_w[0][0:XP_ROWS, 0:TOK], wxp[:, c, :], xc[:, t.s % 2, c, :],
                                   start=c == 0, stop=c == NC - 1)
                mm.then_inc(xproj_done, 1)

            def dt_project(t, c):
                if c == 0:
                    pe.wait_ge(xp_ready, t.idx + 1)
                if t.after(1) or c > 1:
                    pe.wait_ge(dt_ready, t.idx * NC + c - 1)
                pe.matmul(ps_d[c % 2][:, 0:TOK], wdt[:, c * P:(c + 1) * P], xp[0:DTR, :],
                          start=True, stop=True).then_inc(dtp_done, 1)

            def dtn_project(t):
                pe.wait_ge(dt_ready, t.idx * NC + NC)
                if t.after(1):
                    pe.wait_ge(sz_ready, t.idx * NG)
                if t.after(2):
                    pe.wait_ge(res_added, t.idx * KT - 2 * KT + 2)
                for c in range(NC):
                    mm = pe.matmul(ps_w[0][0:B_ROW + NS, 0:TOK], wdtn[:, c, :], dt[:, c, :],
                                   start=c == 0, stop=c == NC - 1)
                mm.then_inc(dtn_done, 1)

            def sum_states(i, st):
                g, q = st // QS, st % QS
                bank = ps_y[g % 2]
                if q == 0:
                    if i.after(1) or g > 1:
                        pe.wait_ge(y_ready, i.idx * NG + g - 1)
                    pe.wait_ge(x4_loaded[g % 2], i.idx * (8 * SEM_DMA) + (g // 2 + 1) * 4 * SEM_DMA)
                    for c in range(NC):
                        mm = pe.matmul(bank[32 * c:32 * c + 32, 0:TOK], skip_w[:, g, c, :], x4[:, g % 2, c, :],
                                       start=True, stop=False, skip_group_check=True)
                    mm.then_inc(skip_added, QS)
                pe.wait_ge(g_ready, i.idx * STEPS + st + 1)
                for c in range(NC):
                    mm = pe.matmul(bank[32 * c:32 * c + 32, 0:TOK], nsum[:], uhg[:, st % RING, c, :],
                                   start=False, stop=q == QS - 1, skip_group_check=True)
                mm.then_inc(g_used, 1)

            def y_mean(t):
                pe.wait_ge(y_ready, t.idx * NG + NG)
                if t.at(1).exists():
                    pe.wait_ge(db_ready, t.idx + 2)
                if t.after(1):
                    pe.wait_ge(res_added, t.idx * KT - KT + 2)
                for g in range(NG):
                    mm = pe.matmul(ps_w[0][:, 0:TOK], mean_w[:], y[:, t.s % 2, g, :], start=g == 0, stop=g == NG - 1)
                mm.then_inc(mean_done, 1)

            def y_var(t):
                pe.wait_ge(sz_ready, t.idx * NG + 3)
                if t.after(1):
                    pe.wait_ge(res_added, t.idx * KT)
                for g in range(NG):
                    pe.wait_ge(squared, t.idx * NG + g + 1)
                    pe.matmul(ps_w[1][:, 0:TOK], mean_w[:], sq[:, g % 2, :],
                              start=g == 0, stop=g == NG - 1).then_inc(sq_used, 1)

            def z_project(t, g):
                bank = ps_w[1 - g % 2]
                if g == 0:
                    pe.wait_ge(xlnT_ready, t.idx * KM + KM)
                    if t.after(1):
                        pe.wait_ge(rstd_ready, t.idx)
                elif g == 1:
                    if t.at(1).exists():
                        pe.wait_ge(xp_ready, t.idx + 2)
                    if t.after(1):
                        pe.wait_ge(centred, t.idx)
                else:
                    pe.wait_ge(sz_ready, t.idx * NG + g - 1)
                for m in range(KM):
                    mm = pe.matmul(bank[:, 0:TOK], win[:, m, DI + g * P:DI + (g + 1) * P],
                                   xlnT[:, t.s % XLN_TILES, m, :], start=m == 0, stop=m == KM - 1)
                mm.then_inc(z_done, 1)

            def out_project(t, k):
                bank = ps_w[1 - k % 2]
                nxt = t.at(1)
                if k == 0:
                    pe.wait_ge(gated, t.idx * NG + NG)
                    pe.wait_ge(rstd_ready, t.idx + 1)
                    if nxt.exists():
                        pe.wait_ge(sz_ready, nxt.idx * NG + 3)
                elif k == 1:
                    pe.wait_ge(centred, t.idx + 1)
                    if nxt.exists():
                        pe.wait_ge(sz_ready, nxt.idx * NG + 4)
                else:
                    pe.wait_ge(res_added, t.idx * KT + 1)
                for g in range(NG):
                    pe.matmul(bank[:, 0:DM], y[:, t.s % 2, g, k * P:(k + 1) * P], wout[:, g, :],
                              start=g == 0, stop=False)
                pe.matmul(bank[:, 0:DM], ones_row[:], bout[:], start=False, stop=True).then_inc(out_done, 1)

            def body(b):
                for s in range(TPB):
                    i = Tile(b, s)
                    prev, nxt, ahead = i.at(-1), i.at(1), i.at(3)
                    for st in range(STEPS):
                        if nxt.exists() and st < 6:
                            newest = nxt.at(1) if nxt.at(1).exists() else nxt
                            conv(nxt, 6 * st, 6 * st + 6, newest)
                        if st == 4 and prev.exists():
                            y_mean(prev)
                        if st == 7:
                            if nxt.exists():
                                x_project(nxt)
                            if prev.exists():
                                y_var(prev)
                        if st == 9 and nxt.exists():
                            dt_project(nxt, 0)
                            dt_project(nxt, 1)
                        if st == 10:
                            z_project(i, 0)
                            z_project(i, 1)
                        if st == 11:
                            if nxt.exists():
                                dt_project(nxt, 2)
                                dt_project(nxt, 3)
                            z_project(i, 2)
                            z_project(i, 3)
                        if st == 12 and ahead.exists():
                            transpose_x(ahead, lambda m: pe.wait_ge(xc_ready, nxt.idx * NC + 3 + m))
                        if st == 13 and prev.exists():
                            out_project(prev, 0)
                            out_project(prev, 1)
                        if st == 14 and nxt.exists():
                            dtn_project(nxt)
                        if st == 14 and prev.exists():
                            out_project(prev, 2)
                        if st == 14 and ahead.exists():
                            project(ahead, 0)
                            project(ahead, 1)
                        if st == 15 and ahead.exists():
                            project(ahead, 2)
                            project(ahead, 3)
                        if st >= 2:
                            sum_states(i, st - 2)
                        elif prev.exists():
                            sum_states(prev, st + STEPS - 2)

            pe.wait_ge(weights_in, WEIGHT_DMAS * SEM_DMA)
            pe.wait_ge(masks_set, 1)
            pe.wait_ge(consts_set, 1)
            pe.wait_ge(pads_set, 1)
            for s in range(3):
                t = Tile(0, s)
                if s == 0:
                    transpose_x(t, lambda m: None)
                else:
                    transpose_x(t, lambda m: pe.wait_ge(xh_ready, t.idx * NC - 1 + m))
                for c in range(NC):
                    project(t, c)
            conv(Tile(0, 0), 0, 9 * NC, Tile(0, 2))
            x_project(Tile(0, 0))
            for c in range(NC):
                dt_project(Tile(0, 0), c)
            dtn_project(Tile(0, 0))
            body(0)
            with pe.Fori(1, IMAGES - 1) as b:
                body(b)
            body(IMAGES - 1)
            last = Tile(IMAGES - 1, TPB - 1)
            sum_states(last, STEPS - 2)
            sum_states(last, STEPS - 1)
            y_mean(last)
            y_var(last)
            for k in range(KT):
                out_project(last, k)

        @block.scalar
        def _(act):
            def decay(i, st):
                g, q = st // QS, st % QS
                if q == 0:
                    act.wait_ge(dt4_loaded[g % 2], i.idx * (8 * SEM_DMA) + (g // 2 + 1) * 4 * SEM_DMA)
                if i.after(1) or st > 1:
                    act.wait_ge(h_ready, i.idx * STEPS + st - 1)
                act.activation(a[:, st % 2], dt4[:, g % 2], ACT.Exp, scale=a4[:, q:q + 1]).then_inc(a_ready, 1)

            def inv_sqrt(var, dst, eps, dst_log_sem, log_count, done_sem):
                act.activation(dst, var, ACT.Ln, bias=eps).then_inc(dst_log_sem, 1)
                act.wait_ge(dst_log_sem, log_count)
                act.activation(dst, dst, ACT.Exp, scale=-0.5).then_inc(done_sem, 1)

            def ln1_scale(t):
                act.wait_ge(ln1_var, t.idx + 1)
                if t.after(1):
                    act.wait_ge(xln_ready, t.idx)
                inv_sqrt(mv1[:, :, 1], rs1[:], eps1[:], ln1_log, t.idx + 1, ln1_rstd)

            def ln2_scale(t):
                act.wait_ge(ln2_var, t.idx + 1)
                if t.after(1):
                    act.wait_ge(final_ready, t.idx)
                inv_sqrt(mv2[:, :, 1], rs2[:], eps2[:], ln2_log, t.idx + 1, ln2_rstd)

            def copy_xlnT(t):
                for m in range(KM):
                    act.wait_ge(xt_done, t.idx * KM + m + 1)
                    if t.after(3) and m == 0:
                        act.wait_ge(z_done, t.idx * NG - 2 * NG)
                    act.activation(xlnT[:, t.s % XLN_TILES, m, :], ps_c[m][:, 0:TOK], ACT.Copy).then_inc(xlnT_ready, 1)

            def copy_xh(t, c):
                act.wait_ge(proj_done, t.idx * NC + c + 1)
                if t.after(3) and c == 0:
                    act.wait_ge(conv_done, t.idx * NC - NC)
                slot = t.s % XH_TILES
                act.activation(xh[:, c, slot * ROWS:(slot + 1) * ROWS, 1:1 + SIDE],
                               ps_c[c % 2][:, 0:TOK].rearrange("p (r w) -> p r w", r=ROWS), ACT.Copy) \
                   .then_inc(xh_ready, 1)

            def copy_xc(t, c):
                act.wait_ge(conv_done, t.idx * NC + c + 1)
                if t.after(2) and c == 0:
                    for n in range(2):
                        act.wait_ge(x4_loaded[n], t.idx * (8 * SEM_DMA) - 8 * SEM_DMA)
                act.activation(xc[:, t.s % 2, c, :], ps_c[c % 2][:, 0:TOK], ACT.Copy).then_inc(xc_ready, 1)

            def copy_xp(t):
                act.wait_ge(xproj_done, t.idx + 1)
                if t.after(1):
                    act.wait_ge(dtp_done, t.idx * NC)
                    act.wait_ge(db_ready, t.idx)
                    act.wait_ge(bounced, t.idx * (2 * SEM_DMA))
                act.activation(xp[:], ps_w[0][0:XP_ROWS, 0:TOK], ACT.Copy).then_inc(xp_ready, 1)

            def softplus_exp(t, c):
                act.wait_ge(clamped, t.idx * NC + c + 1)
                act.activation(spt[:, c % 2, :], spt[:, c % 2, :], ACT.Exp).then_inc(sp_exp, 1)

            def softplus_log(t, c):
                act.wait_ge(sp_exp, t.idx * NC + c + 1)
                act.activation(spt[:, c % 2, :], spt[:, c % 2, :], ACT.Ln, bias=one_c[:]).then_inc(sp_log, 1)

            def copy_y(i, g):
                act.wait_ge(g_used, i.idx * STEPS + QS * (g + 1))
                if i.after(2) and g == 0:
                    act.wait_ge(out_done, i.idx * KT - KT)
                act.activation(y[:, i.s % 2, g, :], ps_y[g % 2][:, 0:TOK], ACT.Copy).then_inc(y_ready, 1)

            def square(t, g):
                if g == 0:
                    act.wait_ge(centred, t.idx + 1)
                if t.after(1) or g > 1:
                    act.wait_ge(sq_used, t.idx * NG + g - 1)
                act.activation(sq[:, g % 2, :], y[:, t.s % 2, g, :], ACT.Square).then_inc(squared, 1)

            def y_scale(t):
                act.wait_ge(sq_used, t.idx * NG + NG)
                if t.after(1):
                    act.wait_ge(normed, t.idx * NG)
                inv_sqrt(ps_w[1][:, 0:TOK], rstd[:], eps2[:], var_log, t.idx + 1, rstd_ready)

            def gate(t, g):
                if t.after(1) and g == 0:
                    act.wait_ge(gated, t.idx * NG)
                act.wait_ge(z_done, t.idx * NG + g + 1)
                act.activation(sz[:, g, :], ps_w[1 - g % 2][:, 0:TOK], ACT.Silu).then_inc(sz_ready, 1)

            def body(b):
                for s in range(TPB):
                    i = Tile(b, s)
                    prev, nxt, ahead = i.at(-1), i.at(1), i.at(3)
                    for st in range(STEPS):
                        decay(i, st)
                        if nxt.exists():
                            for c, when in enumerate((2, 3, 5, 6)):
                                if st == when:
                                    copy_xc(nxt, c)
                            if st == 8:
                                copy_xp(nxt)
                            if st == 10:
                                softplus_exp(nxt, 0)
                                softplus_exp(nxt, 1)
                                softplus_log(nxt, 0)
                                softplus_log(nxt, 1)
                            if st == 12:
                                softplus_exp(nxt, 2)
                                softplus_exp(nxt, 3)
                                softplus_log(nxt, 2)
                                softplus_log(nxt, 3)
                        if prev.exists():
                            if st == 2:
                                copy_y(prev, 3)
                            if st == 6:
                                square(prev, 0)
                                square(prev, 1)
                            if st == 7:
                                square(prev, 2)
                                square(prev, 3)
                            if st == 8:
                                y_scale(prev)
                            if st == 15:
                                ln2_scale(prev)
                        if st in (6, 10, 14):
                            copy_y(i, (st - 6) // 4)
                        if st == 11:
                            for g in range(NG):
                                gate(i, g)
                        if ahead.exists():
                            if st == 5:
                                ln1_scale(ahead)
                            if st == 13:
                                copy_xlnT(ahead)
                            if st == 14:
                                copy_xh(ahead, 0)
                                copy_xh(ahead, 1)
                            if st == 15:
                                copy_xh(ahead, 2)
                                copy_xh(ahead, 3)

            act.wait_ge(weights_in, WEIGHT_DMAS * SEM_DMA)
            act.wait_ge(consts_set, 1)
            act.activation(a4[:], a4[:], ACT.Exp).then_inc(a_exp, 1)
            for s in range(3):
                ln1_scale(Tile(0, s))
                copy_xlnT(Tile(0, s))
                for c in range(NC):
                    if s == 0 and c == 0:
                        act.wait_ge(pads_set, 1)
                    copy_xh(Tile(0, s), c)
            t = Tile(0, 0)
            for c in range(NC):
                copy_xc(t, c)
            copy_xp(t)
            for c in range(NC):
                softplus_exp(t, c)
                softplus_log(t, c)
            act.wait_ge(masks_set, 2)
            body(0)
            with act.Fori(1, IMAGES - 1) as b:
                body(b)
            body(IMAGES - 1)
            last = Tile(IMAGES - 1, TPB - 1)
            copy_y(last, 3)
            for g in range(NG):
                square(last, g)
            y_scale(last)
            ln2_scale(last)

        FFN = 14

        @block.vector
        def _(dve):
            def step_input(i, st):
                g, q = st // QS, st % QS
                if q == 0:
                    dve.wait_ge(x4_loaded[g % 2], i.idx * (8 * SEM_DMA) + (g // 2 + 1) * 4 * SEM_DMA)
                if st == 0:
                    dve.wait_ge(db4_loaded[i.s % 2], i.half * (4 * SEM_DMA) + 4 * SEM_DMA)
                if i.after(1) or st >= RING:
                    dve.wait_ge(g_used, i.idx * STEPS + st - RING + 1)
                dve.tensor_tensor(uhg[:, st % RING], x4[:, g % 2],
                                  db4[:, i.s % 2, q:q + 1, :].broadcast_to([P, NC, TOK]), ALU.mult) \
                   .then_inc(u_ready, 1)

            def recur(i, st):
                dve.wait_ge(u_ready, i.idx * STEPS + st + 1)
                dve.wait_ge(a_ready, i.idx * STEPS + st + 1)
                if not i.first_of_image():
                    dve.wait_ge(carry_saved, i.idx * STEPS - STEPS + st + 1)
                for c in range(NC):
                    h0 = 0.0 if i.first_of_image() else carry[:, st, c:c + 1]
                    ins = dve.tensor_tensor_scan(uhg[:, st % RING, c, :], a[:, st % 2, c, :], uhg[:, st % RING, c, :],
                                                 h0, ALU.mult, ALU.add)
                ins.then_inc(h_ready, 1)

            def ln1_stats(t):
                dve.wait_ge(xin_loaded, t.idx * SEM_DMA + SEM_DMA)
                for k in range(KT):
                    ins = dve.bn_stats(st1[:, k, :], xin[:, k, :])
                ins.then_inc(ln1_stat, 1)

            def ln1_aggregate(t):
                dve.wait_ge(ln1_stat, t.idx + 1)
                dve.memset(wait_pad1[:], 0.0)
                for k in range(KT):
                    ins = dve.bn_aggr(mv1[:, k, :], st1[:, k, :])
                ins.then_inc(ln1_var, 1)

            def ln1_apply(t):
                dve.wait_ge(ln1_var, t.idx + 1)
                dve.wait_ge(ln1_rstd, t.idx + 1)
                for k in range(KT):
                    ins = dve.tensor_scalar(xin[:, k, :], xin[:, k, :], mv1[:, k, 0:1], rs1[:, k:k + 1],
                                            ALU.subtract, ALU.mult)
                ins.then_inc(xln_ready, 1)

            def clamp_dt(t, c):
                dve.wait_ge(dtp_done, t.idx * NC + c + 1)
                dve.tensor_scalar(spt[:, c % 2, :], ps_d[c % 2][:, 0:TOK], bdt[:, c:c + 1], DT_CLAMP,
                                  ALU.add, ALU.min).then_inc(clamped, 1)

            def finish_dt(t, c):
                dve.wait_ge(sp_log, t.idx * NC + c + 1)
                if t.after(1) and c == 0:
                    for n in range(2):
                        dve.wait_ge(dt4_loaded[n], t.idx * (8 * SEM_DMA))
                    dve.wait_ge(dtn_done, t.idx)
                dve.scalar_tensor_tensor(dt[:, c, :], ps_d[c % 2][:, 0:TOK], bdt[:, c:c + 1], spt[:, c % 2, :],
                                         ALU.add, ALU.max).then_inc(dt_ready, 1)

            def make_db(t):
                dve.wait_ge(dtn_done, t.idx + 1)
                dve.wait_ge(xp_ready, t.idx + 1)
                if t.after(1):
                    dve.wait_ge(bounced, t.idx * (2 * SEM_DMA))
                rows = slice(B_ROW, B_ROW + NS)
                dve.scalar_tensor_tensor(dbt[rows, :], ps_w[0][rows, 0:TOK], bdtn[rows, :], xp[rows, :],
                                         ALU.add, ALU.mult).then_inc(db_ready, 1)

            def centre(t):
                dve.wait_ge(mean_done, t.idx + 1)
                ys = y[:, t.s % 2]
                mean = ps_w[0][:, 0:TOK].unsqueeze(1).broadcast_to([P, NG, TOK])
                dve.tensor_tensor(ys, ys, mean, ALU.subtract).then_inc(centred, 1)

            def norm(t, g):
                if g == 0:
                    dve.wait_ge(rstd_ready, t.idx + 1)
                    dve.wait_ge(centred, t.idx + 1)
                ys = y[:, t.s % 2, g, :]
                dve.scalar_tensor_tensor(ys, ys, gam[:, g:g + 1], rstd[:], ALU.mult, ALU.mult).then_inc(normed, 1)

            def gate_y(t, g):
                dve.wait_ge(normed, t.idx * NG + g + 1)
                dve.wait_ge(sz_ready, t.idx * NG + g + 1)
                ys = y[:, t.s % 2, g, :]
                dve.scalar_tensor_tensor(ys, ys, bet[:, g:g + 1], sz[:, g, :], ALU.add, ALU.mult).then_inc(gated, 1)

            def add_residual(t, k):
                if k == 0:
                    dve.wait_ge(res_loaded, t.idx * SEM_DMA + SEM_DMA)
                dve.wait_ge(out_done, t.idx * KT + k + 1)
                dve.tensor_tensor(res[:, k, :], res[:, k, :], ps_w[1 - k % 2][:, 0:DM], ALU.add).then_inc(res_added, 1)

            def ln2_stats(t):
                dve.wait_ge(res_added, t.idx * KT + KT)
                for k in range(KT):
                    ins = dve.bn_stats(st2[:, k, :], res[:, k, :])
                ins.then_inc(ln2_stat, 1)

            def ln2_aggregate(t):
                dve.wait_ge(ln2_stat, t.idx + 1)
                dve.memset(wait_pad2[:], 0.0)
                for k in range(KT):
                    ins = dve.bn_aggr(mv2[:, k, :], st2[:, k, :])
                ins.then_inc(ln2_var, 1)

            def ffn_stage(t, n):
                if n == 0:
                    dve.wait_ge(ln2_rstd, t.idx + 1)
                    dve.wait_ge(ln2_var, t.idx + 1)
                else:
                    dve.wait_ge(ffn, t.idx * FFN + n)
                if n == 0:
                    for k in range(KT):
                        dve.tensor_scalar(hot[:, k, :], res[:, k, 0:64], mv2[:, k, 0:1], rs2[:, k:k + 1],
                                          ALU.subtract, ALU.mult)
                    dve.tensor_scalar(sc1[:], rs2[:], 1.0, None, ALU.add)
                    ins = dve.tensor_tensor(sc2[:], rs2[:], mv2[:, :, 0], ALU.mult)
                elif n == 1:
                    for k in range(KT):
                        dve.tensor_scalar(res[:, k, :], res[:, k, :], sc1[:, k:k + 1], sc2[:, k:k + 1],
                                          ALU.mult, ALU.subtract)
                    ins = dve.tensor_scalar(hot[:], hot[:], 0.5, None, ALU.is_gt)
                elif n == 2:
                    for w in range(3):
                        dve.tensor_tensor(score[:, :, w, :], hot[:, :, 32 + 8 * w:48 + 8 * w],
                                          score16[:].unsqueeze(1).broadcast_to([P, KT, 16]), ALU.mult)
                    ins = dve.tensor_tensor(amp[:], hot[:, :, 39], hot[:, :, 40], ALU.max)
                elif n == 3:
                    dve.scalar_tensor_tensor(amp[:], amp[:], 2.0, hot[:, :, 0], ALU.mult, ALU.mult)
                    ins = dve.tensor_reduce(best[:], score[:], AX_X, ALU.max)
                elif n == 4:
                    ins = dve.tensor_scalar(found[:], best[:], 0.0, None, ALU.is_gt)
                elif n == 5:
                    ins = dve.tensor_scalar(best[:], best[:], -1.0, 16.0, ALU.mult, ALU.add)
                elif n == 6:
                    ins = dve.tensor_tensor(nib[:], best[:], found[:], ALU.mult)
                elif n == 7:
                    ins = dve.scalar_tensor_tensor(val[:], nib[:, :, 1], 16.0, nib[:, :, 0], ALU.mult, ALU.add)
                elif n == 8:
                    dve.tensor_tensor(shl[:], val[:], nib[:, :, 2], ALU.logical_shift_left)
                    ins = dve.tensor_tensor(shr[:], val[:], nib[:, :, 2], ALU.logical_shift_right)
                elif n == 9:
                    ins = dve.tensor_single_scalar(shl[:], shl[:], 255, ALU.bitwise_and)
                elif n == 10:
                    ins = dve.tensor_tensor(dif[:], shl[:], shr[:], ALU.subtract)
                elif n == 11:
                    ins = dve.tensor_tensor(dif[:], dif[:], hot[:, :, 39], ALU.mult)
                elif n == 12:
                    ins = dve.tensor_tensor(resi[:], dif[:], shr[:], ALU.add)
                elif n == 13:
                    dve.tensor_single_scalar(rnib[:, :, 0], resi[:], 15, ALU.bitwise_and)
                    ins = dve.tensor_single_scalar(rnib[:, :, 1], resi[:], 4, ALU.logical_shift_right)
                ins.then_inc(ffn, 1)

            def ffn_mark(t):
                dve.wait_ge(ffn, t.idx * FFN + FFN)
                for w in range(2):
                    ins = dve.tensor_tensor(hots[:, :, w, :], rnib[:, :, w:w + 1].broadcast_to([P, KT, 16]),
                                            idx16[:].unsqueeze(1).broadcast_to([P, KT, 16]), ALU.is_equal)
                ins.then_inc(marked, 1)

            def ffn_weigh(t):
                dve.wait_ge(marked, t.idx * 3 + 1)
                for w in range(2):
                    ins = dve.tensor_tensor(hots[:, :, w, :], hots[:, :, w, :],
                                            amp[:].unsqueeze(2).broadcast_to([P, KT, 16]), ALU.mult)
                ins.then_inc(marked, 1)

            def ffn_add_low(t):
                dve.wait_ge(marked, t.idx * 3 + 2)
                dve.tensor_tensor(res[:, :, 64:80], res[:, :, 64:80], hots[:, :, 0, :], ALU.add).then_inc(marked, 1)

            def ffn_add_high(t):
                dve.wait_ge(marked, t.idx * 3 + 3)
                dve.tensor_tensor(res[:, :, 72:88], res[:, :, 72:88], hots[:, :, 1, :], ALU.add) \
                   .then_inc(final_ready, 1)

            def body(b):
                for s in range(TPB):
                    i = Tile(b, s)
                    before, prev, nxt, ahead = i.at(-2), i.at(-1), i.at(1), i.at(3)
                    for st in range(STEPS):
                        if st + 1 < STEPS:
                            step_input(i, st + 1)
                        if before.exists():
                            if st < 5:
                                ffn_stage(before, 2 * st)
                        if prev.exists():
                            if st == 5:
                                centre(prev)
                            if st == 9:
                                for g in range(NG):
                                    norm(prev, g)
                            if st == 10:
                                for g in range(NG):
                                    gate_y(prev, g)
                            if st == 13:
                                add_residual(prev, 0)
                                add_residual(prev, 1)
                            if st == 14:
                                add_residual(prev, 2)
                            if st == 15:
                                ln2_aggregate_after_stats(prev)
                        if nxt.exists():
                            if st == 9:
                                clamp_dt(nxt, 0)
                                clamp_dt(nxt, 1)
                            if st == 11:
                                finish_dt(nxt, 0)
                                finish_dt(nxt, 1)
                                clamp_dt(nxt, 2)
                                clamp_dt(nxt, 3)
                            if st == 13:
                                finish_dt(nxt, 2)
                                finish_dt(nxt, 3)
                            if st == 15:
                                make_db(nxt)
                        if ahead.exists():
                            if st == 3:
                                ln1_stats(ahead)
                            if st == 4:
                                ln1_aggregate(ahead)
                            if st == 6:
                                ln1_apply(ahead)
                        recur(i, st)
                        if before.exists():
                            if st < 5 :
                                ffn_stage(before, 2 * st + 1)
                            elif st == 5:
                                ffn_stage(before, 10)
                                ffn_stage(before, 11)
                            elif st == 6:
                                ffn_stage(before, 12)
                            elif st == 7:
                                ffn_stage(before, 13)
                            elif st == 8:
                                ffn_mark(before)
                            elif st == 9:
                                ffn_weigh(before)
                            elif st == 10:
                                ffn_add_low(before)
                            elif st == 11:
                                ffn_add_high(before)
                    if nxt.exists():
                        step_input(nxt, 0)

            def ln2_aggregate_after_stats(t):
                ln2_stats(t)
                ln2_aggregate(t)

            def finish(t):
                for n in range(FFN):
                    ffn_stage(t, n)
                ffn_mark(t)
                ffn_weigh(t)
                ffn_add_low(t)
                ffn_add_high(t)

            dve.memset(wxp[:], 0.0).then_inc(zeros_set, 1)
            dve.memset(wdtn[:], 0.0).then_inc(zeros_set, 1)
            dve.memset(xh[:, :, :, 0:1], 0.0)
            dve.memset(xh[:, :, :, SIDE + 1:SIDE + 2], 0.0).then_inc(pads_set, 1)
            dve.memset(mean_w[:], 1.0 / DI)
            dve.memset(ones_row[:], 1.0)
            dve.memset(one_c[:], 1.0)
            dve.memset(eps1[:], 1e-6)
            dve.memset(eps2[:], 1e-5).then_inc(consts_set, 1)
            dve.wait_ge(ident_set, 2)
            dve.wait_ge(nsum_set, 5)
            dve.wait_ge(weights_in, WEIGHT_DMAS * SEM_DMA)
            for c in range(NC):
                for w in range(9):
                    dve.tensor_scalar(conv_w[:, c, w, :], ident[:], taps[:, c, w:w + 1], None, ALU.mult)
            for g in range(NG):
                for c in range(NC):
                    ins = dve.tensor_scalar(skip_w[:, g, c, :], nsum[:], dskip4[:, g, c:c + 1], 0.25,
                                            ALU.mult, ALU.mult)
            ins.then_inc(masks_set, 1)
            dve.wait_ge(a_exp, 1)
            dve.tensor_scalar(a4[:], a4[:], -1.0, None, ALU.mult).then_inc(masks_set, 1)
            dve.wait_ge(idx_set, 2)
            for s in range(3):
                ln1_stats(Tile(0, s))
                ln1_aggregate(Tile(0, s))
                ln1_apply(Tile(0, s))
            t = Tile(0, 0)
            clamp_dt(t, 0)
            clamp_dt(t, 1)
            for c in range(NC):
                finish_dt(t, c)
                if c < 2:
                    clamp_dt(t, c + 2)
            make_db(t)
            step_input(t, 0)
            body(0)
            with dve.Fori(1, IMAGES - 1) as b:
                body(b)
            body(IMAGES - 1)
            last = Tile(IMAGES - 1, TPB - 1)
            finish(last.at(-1))
            centre(last)
            for g in range(NG):
                norm(last, g)
            for g in range(NG):
                gate_y(last, g)
            for k in range(KT):
                add_residual(last, k)
            ln2_stats(last)
            ln2_aggregate(last)
            finish(last)

        @block.gpsimd
        def _(pool):
            def weigh(i, st):
                q = st % QS
                pool.wait_ge(h_ready, i.idx * STEPS + st + 1)
                if st == 0:
                    pool.wait_ge(c4_loaded[i.s % 2], i.half * (4 * SEM_DMA) + 4 * SEM_DMA)
                slot = uhg[:, st % RING]
                pool.tensor_tensor(carry[:, st, :], slot[:, :, TOK - 1], one_nc[:], ALU.mult).then_inc(carry_saved, 1)
                pool.wait_ge(carry_saved, i.idx * STEPS + st + 1)
                pool.tensor_tensor(slot, slot, c4[:, i.s % 2, q:q + 1, :].broadcast_to([P, NC, TOK]), ALU.mult) \
                    .then_inc(g_ready, 1)

            def body(b):
                for s in range(TPB):
                    for st in range(STEPS):
                        weigh(Tile(b, s), st)

            pool.memset(one_nc[:], 1.0)
            pool.memset(ident[:], 0.0).then_inc(ident_set, 1)
            pool.wait_ge(ident_set, 1)
            pool.affine_select(out=ident[:], in_=ident[:], compare_op=ALU.not_equal, fill=1.0, base=0,
                               pattern=[[-1, P]], channel_multiplier=1).then_inc(ident_set, 1)
            pool.memset(nsum[:], 0.0).then_inc(nsum_set, 1)
            for k in range(4):
                pool.wait_ge(nsum_set, k + 1)
                pool.affine_select(out=nsum[:], in_=nsum[:], compare_op=ALU.not_equal, fill=1.0, base=-32 * k,
                                   pattern=[[-1, 32]], channel_multiplier=1).then_inc(nsum_set, 1)
            pool.iota(idx16[:], pattern=[[1, 16]], base=0, channel_multiplier=0,
                      allow_small_or_imprecise_dtypes=True).then_inc(idx_set, 1)
            pool.iota(score16[:], pattern=[[-1, 16]], base=16, channel_multiplier=0,
                      allow_small_or_imprecise_dtypes=True).then_inc(idx_set, 1)
            body(0)
            with pool.Fori(1, IMAGES - 1) as b:
                body(b)
            body(IMAGES - 1)


_INS = ['x', 'L0_conv_W_in', 'L0_conv_conv_k', 'L0_conv_W_xproj', 'L0_conv_W_dt', 'L0_conv_b_dt', 'L0_conv_A_log',
        'L0_conv_Dskip', 'L0_conv_W_dtN', 'L0_conv_b_dtN', 'L0_conv_ln_g', 'L0_conv_ln_b', 'L0_conv_W_out',
        'L0_conv_b_out']
_OUTS = [((IMAGES, SIDE, SIDE, DM), 'float32')]


def kernel(**inputs):
    import numpy as _np
    import concourse.bacc as _bacc
    from concourse import mybir as _mybir
    from concourse.bass_utils import run_bass_kernel_spmd as _run

    nc = _bacc.Bacc("TRN2", target_bir_lowering=False, num_devices=1)
    arrays, args = {}, []
    for name in _INS:
        a = _np.ascontiguousarray(inputs[name])
        arrays[f"in_{name}_dram"] = a
        args.append(nc.dram_tensor(f"in_{name}_dram", a.shape, _mybir.dt.from_np(a.dtype), kind="ExternalInput").ap())
    for i, (shape, dtype) in enumerate(_OUTS):
        dt = _mybir.dt.from_np(_np.dtype(dtype))
        args.append(nc.dram_tensor(f"out_{i}_dram", shape, dt, kind="ExternalOutput").ap())
    build(nc, *args)
    r = _run(nc, [arrays], core_ids=[0])
    got = tuple(r.results[0][f"out_{i}_dram"] for i in range(len(_OUTS)))
    return got[0]
```

```python
from contextlib import ExitStack

import concourse.bass as bass
from concourse import mybir

F32 = mybir.dt.float32
I32 = mybir.dt.int32
ALU = mybir.AluOpType
ACT = mybir.ActivationFunctionType
AX_X = mybir.AxisListType.X

P = 128
IMAGES, SIDE, DM = 8, 48, 256
DI, NS, DTR = 512, 16, 8
NC = DI // P
KM = DM // P
ROWS = 8
TOK = ROWS * SIDE
KT = TOK // P
TPB = SIDE // ROWS
TILES = IMAGES * TPB
BLOCKS = DI // 32
POOL_Q = 3
QS = 4
NG = 4
STEPS = NG * QS
RING = 4
XH_TILES = 3
XLN_TILES = 3
SEM_DMA = 16
B_ROW, C_ROW = 32, 64
XP_ROWS = 96


class Tile:

    def __init__(self, b, s):
        self.b, self.s = b, s
        self.idx = b * TPB + s
        self.half = b * (TPB // 2) + s // 2

    def at(self, n):
        return Tile(self.b, self.s + n)

    def exists(self):
        return not isinstance(self.b, int) or 0 <= self.idx < TILES

    def after(self, n):
        return not isinstance(self.b, int) or self.idx >= n

    def first_of_image(self):
        return self.s % TPB == 0

    def last_of_image(self):
        return self.s % TPB == TPB - 1


def carries(t, st):
    return t.b * ((TPB - 1) * STEPS) + t.s * STEPS + st + 1


def stack_parts(t):
    slot = t.s % XH_TILES
    r0, end = slot * ROWS, XH_TILES * ROWS
    if t.first_of_image():
        above = [(0, 0, None, 1), (0, 1, r0, ROWS - 1)]
    elif slot == 0:
        above = [(0, 0, end - 1, 1), (0, 1, r0, ROWS - 1)]
    else:
        above = [(0, 0, r0 - 1, ROWS)]
    if t.last_of_image():
        below = [(2, 0, r0 + 1, ROWS - 1), (2, ROWS - 1, None, 1)]
    elif slot == XH_TILES - 1:
        below = [(2, 0, r0 + 1, ROWS - 1), (2, ROWS - 1, 0, 1)]
    else:
        below = [(2, 0, r0 + 1, ROWS)]
    half = ROWS // 2
    whole = len(above) + len(below) > 2
    centre = [(1, 0, r0, ROWS)] if whole else [(1, 0, r0, half), (1, half, r0 + half, half)]
    return above + centre + below


def build(nc, x, W_in, conv_k, W_xproj, W_dt, b_dt, A_log, Dskip, W_dtN, b_dtN, ln_g, ln_b, W_out, b_out, out):
    x_tiles = x.rearrange("b (s r) w m -> (b s) (r w) m", r=ROWS).rearrange("i (k p) m -> i p k m", p=P)
    out_tiles = out.rearrange("b (s r) w m -> (b s) (r w) m", r=ROWS).rearrange("i (k p) m -> i p k m", p=P)

    with ExitStack() as ctx:
        def sb(name, shape, dt=F32):
            return ctx.enter_context(nc.sbuf_tensor(name, shape, dt))

        def pb(name):
            return ctx.enter_context(nc.psum_tensor(name, [P, 512], F32))

        def sem(name):
            return ctx.enter_context(nc.semaphore(name))

        win = sb("win", [P, KM, 2 * DI])
        wout = sb("wout", [P, NC, DM])
        wxp = sb("wxp", [P, NG, XP_ROWS])
        wdt = sb("wdt", [DTR + 1, DI])
        wdtn = sb("wdtn", [P, NG, B_ROW + NS])
        taps = sb("taps", [P, 3, BLOCKS])
        conv_w = sb("conv_w", [P, 3, BLOCKS, 32])
        ident = sb("ident", [P, P])
        mean_w = sb("mean_w", [P, P])
        nsum = sb("nsum", [P, 32])
        skip_w = sb("skip_w", [P, NG, NC, 32])
        dskip4 = sb("dskip4", [P, NG, NC])
        xp_one = sb("xp_one", [XP_ROWS, 1])
        bdtn = sb("bdtn", [P, 1])
        gam = sb("gam", [P, NG])
        bet = sb("bet", [P, NG])
        a4 = sb("a4", [P, QS])
        bout = sb("bout", [1, DM])
        ones_row = sb("ones_row", [1, P])
        one_c = sb("one_c", [P, 1])
        eps1 = sb("eps1", [P, 1])
        eps2 = sb("eps2", [P, 1])
        one_nc = sb("one_nc", [P, NC])
        idx16 = sb("idx16", [P, 16])
        score16 = sb("score16", [P, 16])
        xin = sb("xin", [P, KT, DM])
        st1 = sb("st1", [P, KT, 6])
        wait_pad1 = sb("wait_pad1", [P, 1])
        wait_pad2 = sb("wait_pad2", [P, 1])
        mv1 = sb("mv1", [P, KT, 2])
        rs1 = sb("rs1", [P, KT])
        xlnT = sb("xlnT", [P, XLN_TILES, KM, TOK])
        xh = sb("xh", [P, NC, XH_TILES * ROWS, SIDE + 2])
        xh4 = sb("xh4", [P, 2, NC, ROWS, SIDE + 2])
        zero_row = sb("zero_row", [32, NC, 1, SIDE + 2])
        xc = sb("xc", [P, 2, NG, TOK])
        xp = sb("xp", [XP_ROWS, TOK])
        dbt = sb("dbt", [B_ROW + NS, TOK])
        dt = sb("dt", [P, NG, TOK])
        dt4 = sb("dt4", [P, 2, NC, TOK])
        x4 = sb("x4", [P, 2, NC, TOK])
        db4 = sb("db4", [P, 2, QS, TOK])
        c4 = sb("c4", [P, 2, QS, TOK])
        a = sb("a", [P, 2, NC, TOK])
        uhg = sb("uhg", [P, RING, NC, TOK])
        carry = sb("carry", [P, STEPS, NC])
        y = sb("y", [P, 2, NG, TOK])
        sq = sb("sq", [P, NG, TOK])
        rstd = sb("rstd", [P, TOK])
        sz = sb("sz", [P, NG, TOK])
        res = sb("res", [P, KT, DM])
        st2 = sb("st2", [P, KT, 6])
        mv2 = sb("mv2", [P, KT, 2])
        rs2 = sb("rs2", [P, KT])
        sc1 = sb("sc1", [P, KT])
        sc2 = sb("sc2", [P, KT])
        hot = sb("hot", [P, KT, 64])
        score = sb("score", [P, KT, 3, 16])
        best = sb("best", [P, KT, 3])
        found = sb("found", [P, KT, 3])
        nib = sb("nib", [P, KT, 3], I32)
        val = sb("val", [P, KT], I32)
        shl = sb("shl", [P, KT], I32)
        shr = sb("shr", [P, KT], I32)
        dif = sb("dif", [P, KT])
        resi = sb("resi", [P, KT], I32)
        rnib = sb("rnib", [P, KT, 2], I32)
        amp = sb("amp", [P, KT])
        hots = sb("hots", [P, KT, 2, 16])

        ps_y = [pb(f"ps_y{n}") for n in range(2)]
        ps_c = [pb(f"ps_c{n}") for n in range(2)]
        ps_d = [pb(f"ps_d{n}") for n in range(2)]
        ps_w = [pb(f"ps_w{n}") for n in range(2)]
        ps_dt = ps_d + ps_c
        ps_out = [ps_w[1], ps_w[0], ps_d[1]]

        bounce = nc.dram_tensor("bounce", [2, 2, NS, TOK], F32, kind="Internal").ap()

        weights_in = sem("weights_in")
        win_in = sem("win_in")
        pads_set = sem("pads_set")
        masks_set = sem("masks_set")
        zeros_set = sem("zeros_set")
        ident_set = sem("ident_set")
        nsum_set = sem("nsum_set")
        idx_set = sem("idx_set")
        a_exp = sem("a_exp")
        consts_set = sem("consts_set")
        xin_loaded = sem("xin_loaded")
        ln1_stat = sem("ln1_stat")
        ln1_var = sem("ln1_var")
        ln1_log = sem("ln1_log")
        ln1_rstd = sem("ln1_rstd")
        xln_ready = sem("xln_ready")
        xt_done = sem("xt_done")
        xlnT_ready = sem("xlnT_ready")
        proj_done = sem("proj_done")
        xh_ready = sem("xh_ready")
        xh4_loaded = [sem(f"xh4_loaded{n}") for n in range(2)]
        conv_done = sem("conv_done")
        xc_ready = sem("xc_ready")
        xproj_done = sem("xproj_done")
        xp_ready = sem("xp_ready")
        dtp_done = sem("dtp_done")
        sp_abs = sem("sp_abs")
        sp_exp = sem("sp_exp")
        sp_log = sem("sp_log")
        dt_ready = sem("dt_ready")
        dtn_done = sem("dtn_done")
        db_ready = sem("db_ready")
        bounced = sem("bounced")
        dt4_loaded = [sem(f"dt4_loaded{n}") for n in range(2)]
        x4_loaded = [sem(f"x4_loaded{n}") for n in range(2)]
        db4_loaded = [sem(f"db4_loaded{n}") for n in range(2)]
        c4_loaded = [sem(f"c4_loaded{n}") for n in range(2)]
        a_ready = sem("a_ready")
        u_ready = sem("u_ready")
        pool_u_ready = sem("pool_u_ready")
        h_ready = sem("h_ready")
        carry_saved = sem("carry_saved")
        g_ready = sem("g_ready")
        g_used = sem("g_used")
        skip_added = sem("skip_added")
        y_ready = sem("y_ready")
        mean_done = sem("mean_done")
        centred = sem("centred")
        squared = sem("squared")
        sq_used = sem("sq_used")
        var_log = sem("var_log")
        rstd_ready = sem("rstd_ready")
        z_done = sem("z_done")
        sz_ready = sem("sz_ready")
        normed = sem("normed")
        gated = sem("gated")
        out_done = sem("out_done")
        res_loaded = sem("res_loaded")
        res_added = sem("res_added")
        ln2_stat = sem("ln2_stat")
        ln2_var = sem("ln2_var")
        ln2_log = sem("ln2_log")
        ln2_rstd = sem("ln2_rstd")
        ffn = sem("ffn")
        marked = sem("marked")
        final_ready = sem("final_ready")
        out_stored = sem("out_stored")

        WEIGHT_DMAS = 3 + 4 * 3 + NG + 1 + NC + 2 + 2 * 4 + 3

        block = ctx.enter_context(nc.Block())

        @block.sync
        def _(sp):
            def load(dst, src):
                sp.dma_start(dst, src, allow_slow_non_contiguous=True).then_inc(weights_in, SEM_DMA)

            def load_weights():
                for y in range(3):
                    load(taps[32 * y:32 * y + 32], conv_k[y, :, 0, :].rearrange("x (b p) -> p x b", p=32))
                sp.wait_ge(zeros_set, 2)
                for c in range(NC):
                    part = slice(32 * c, 32 * c + 32)
                    rows = W_xproj[c * P:(c + 1) * P, :].rearrange("(g p) n -> p g n", g=NG)
                    load(wxp[part, :, 0:DTR], rows[:, :, 0:DTR])
                    load(wxp[part, :, B_ROW:B_ROW + NS], rows[:, :, DTR:DTR + NS])
                    load(wxp[part, :, C_ROW:C_ROW + NS], rows[:, :, DTR + NS:DTR + 2 * NS])
                dt_cols = W_dt.rearrange("r (c g p) -> g r c p", c=NC, g=NG)
                for g in range(NG):
                    load(wdt[0:DTR, g * P:(g + 1) * P].rearrange("r (c p) -> r c p", c=NC), dt_cols[g])
                load(wdt[DTR:DTR + 1, :].rearrange("o (g c p) -> o g c p", g=NG, c=NC),
                     b_dt.rearrange("(o c g p) -> o g c p", o=1, c=NC, g=NG))
                for c in range(NC):
                    part = slice(32 * c, 32 * c + 32)
                    mine = slice(c * P, (c + 1) * P)
                    load(wdtn[part, :, B_ROW:B_ROW + NS], W_dtN[mine, :].rearrange("(g p) n -> p g n", g=NG))
                load(bdtn[B_ROW:B_ROW + NS, :], b_dtN.rearrange("(n o) -> n o", o=1))
                load(bout[:], b_out.rearrange("(o m) -> o m", o=1))
                a_rows = A_log.rearrange("(o q k) -> k o q", o=1, k=4)
                for k in range(4):
                    quad = slice(32 * k, 32 * k + 32)
                    load(a4[quad, :], a_rows[k].broadcast_to([32, QS]))
                    load(dskip4[quad].rearrange("p g c -> p (g c)"), Dskip.rearrange("(b p) -> p b", p=32))
                load(gam[:], ln_g.rearrange("(g p) -> p g", p=P))
                load(bet[:], ln_b.rearrange("(g p) -> p g", p=P))
                load(wout[:], W_out.rearrange("(g p) m -> p g m", p=P))

            def load_stack(t, g):
                buf = g % 2
                newest = t.at(1) if t.at(1).exists() else t
                if g == 0:
                    sp.wait_ge(xh_ready, newest.idx * NC + NC)
                if g > 1:
                    sp.wait_ge(conv_done, t.idx * NG + g - 1)
                for quad, dst_row, src_row, rows in stack_parts(t):
                    dst = xh4[32 * quad:32 * quad + 32, buf, :, dst_row:dst_row + rows, :]
                    src = zero_row[:] if src_row is None else xh[32 * g:32 * g + 32, :, src_row:src_row + rows, :]
                    sp.dma_start(dst, src).then_inc(xh4_loaded[buf], SEM_DMA)

            def load_x(t):
                if t.after(1):
                    sp.wait_ge(xt_done, t.idx * KM)
                sp.dma_start(xin[:], x_tiles[t.idx]).then_inc(xin_loaded, SEM_DMA)

            def load_group(t, g):
                buf = g % 2
                if g == 0:
                    sp.wait_ge(dt_ready, t.idx * NC + NC)
                    sp.wait_ge(xc_ready, t.idx * NC + NC)
                if t.after(1) or g > 1:
                    steps = t.idx * STEPS + QS * (g - 1)
                    sp.wait_ge(a_ready, steps)
                    sp.wait_ge(u_ready, steps)
                    sp.wait_ge(pool_u_ready, steps)
                    sp.wait_ge(skip_added, steps)
                src = slice(32 * g, 32 * g + 32)
                for k in range(4):
                    quad = slice(32 * k, 32 * k + 32)
                    sp.dma_start(dt4[quad, buf], dt[src]).then_inc(dt4_loaded[buf], SEM_DMA)
                for k in range(4):
                    quad = slice(32 * k, 32 * k + 32)
                    sp.dma_start(x4[quad, buf], xc[src, t.s % 2]).then_inc(x4_loaded[buf], SEM_DMA)

            def load_states(t):
                par = t.s % 2
                sp.wait_ge(db_ready, t.idx + 1)
                sp.wait_ge(xp_ready, t.idx + 1)
                if t.after(2):
                    sp.wait_ge(u_ready, t.at(-1).idx * STEPS)
                    sp.wait_ge(pool_u_ready, t.at(-1).idx * STEPS)
                    sp.wait_ge(g_ready, t.at(-1).idx * STEPS)
                    full = t.half * (4 * SEM_DMA)
                    sp.wait_ge(db4_loaded[par], full)
                    sp.wait_ge(c4_loaded[par], full)
                sp.dma_start(bounce[par, 0], dbt[B_ROW:B_ROW + NS, :]).then_inc(bounced, SEM_DMA)
                sp.dma_start(bounce[par, 1], xp[C_ROW:C_ROW + NS, :]).then_inc(bounced, SEM_DMA)
                sp.wait_ge(bounced, t.idx * (2 * SEM_DMA) + 2 * SEM_DMA)
                for which, dst, done in ((0, db4, db4_loaded), (1, c4, c4_loaded)):
                    rows = bounce[par, which].rearrange("(q k) t -> k q t", k=4)
                    for k in range(4):
                        quad = slice(32 * k, 32 * k + 32)
                        sp.dma_start(dst[quad, par], rows[k].unsqueeze(0).broadcast_to([32, QS, TOK])) \
                          .then_inc(done[par], SEM_DMA)

            def load_residual(t):
                if t.after(1):
                    sp.wait_ge(out_stored, t.idx * SEM_DMA)
                sp.dma_start(res[:], x_tiles[t.idx]).then_inc(res_loaded, SEM_DMA)

            def store(t):
                sp.wait_ge(final_ready, t.idx + 1)
                sp.dma_start(out_tiles[t.idx], res[:]).then_inc(out_stored, SEM_DMA)

            def body(b):
                for s in range(TPB):
                    i = Tile(b, s)
                    load_group(i, 1)
                    if i.at(3).exists():
                        load_x(i.at(3))
                    if i.at(1).exists():
                        for g in range(NG):
                            load_stack(i.at(1), g)
                    load_group(i, 2)
                    load_group(i, 3)
                    if i.at(-2).exists():
                        store(i.at(-2))
                    if i.at(-1).exists():
                        load_residual(i.at(-1))
                    if i.at(1).exists():
                        load_group(i.at(1), 0)
                        load_states(i.at(1))

            load_x(Tile(0, 0))
            sp.dma_start(win[:], W_in.rearrange("(k p) n -> p k n", p=P)).then_inc(win_in, SEM_DMA)
            load_x(Tile(0, 1))
            load_weights()
            load_x(Tile(0, 2))
            sp.wait_ge(pads_set, 1)
            for g in range(NG):
                load_stack(Tile(0, 0), g)
            load_group(Tile(0, 0), 0)
            load_states(Tile(0, 0))
            body(0)
            with sp.Fori(1, IMAGES - 1) as b:
                body(b)
            body(IMAGES - 1)
            store(Tile(IMAGES - 1, TPB - 2))
            load_residual(Tile(IMAGES - 1, TPB - 1))
            store(Tile(IMAGES - 1, TPB - 1))
            sp.wait_ge(out_stored, TILES * SEM_DMA)
            sp.wait_ge(bounced, TILES * 2 * SEM_DMA)

        @block.tensor
        def _(pe):
            def transpose_x(t, ps_free):
                pe.wait_ge(xln_ready, t.idx + 1)
                for m in range(KM):
                    ps_free(m)
                    for k in range(KT):
                        mm = pe.transpose(ps_c[m][:, k * P:(k + 1) * P], xin[:, k, m * P:(m + 1) * P], ident[:])
                    mm.then_inc(xt_done, 1)

            def project(t, c):
                if c == 0:
                    pe.wait_ge(xlnT_ready, t.idx * KM + KM)
                if c >= 2:
                    pe.wait_ge(xh_ready, t.idx * NC + c - 1)
                for m in range(KM):
                    mm = pe.matmul(ps_c[c % 2][:, 0:TOK], win[:, m, c * P:(c + 1) * P], xlnT[:, t.s % XLN_TILES, m, :],
                                   start=m == 0, stop=m == KM - 1)
                mm.then_inc(proj_done, 1)

            def conv(t, g, newest):
                if g < 2:
                    pe.wait_ge(xh_ready, newest.idx * NC + g + 3)
                else:
                    pe.wait_ge(xc_ready, t.idx * NG + g - 1)
                pe.wait_ge(xh4_loaded[g % 2], t.idx * (8 * SEM_DMA) + (g // 2 + 1) * 4 * SEM_DMA)
                for dx in range(3):
                    for c in range(NC):
                        mm = pe.matmul(ps_c[g % 2][32 * c:32 * c + 32, 0:TOK], conv_w[:, dx, NG * c + g, :],
                                       xh4[:, g % 2, c, :, dx:dx + SIDE], start=dx == 0, stop=dx == 2,
                                       skip_group_check=True)
                mm.then_inc(conv_done, 1)

            def x_project(t):
                pe.wait_ge(xc_ready, t.idx * NG + NG)
                if t.after(2):
                    pe.wait_ge(centred, t.idx - 1)
                for g in range(NG):
                    mm = pe.matmul(ps_w[0][0:XP_ROWS, 0:TOK], wxp[:, g, :], xc[:, t.s % 2, g, :],
                                   start=g == 0, stop=g == NG - 1)
                mm.then_inc(xproj_done, 1)

            def dt_project(t):
                pe.wait_ge(xp_ready, t.idx + 1)
                if t.after(1):
                    pe.wait_ge(db_ready, t.idx)
                if t.after(3):
                    pe.wait_ge(res_added, t.idx * KT - 2 * KT)
                for g in range(NG):
                    pe.matmul(ps_dt[g][:, 0:TOK], wdt[:, g * P:(g + 1) * P], xp[0:DTR + 1, :],
                              start=True, stop=True).then_inc(dtp_done, 1)

            def dtn_project(t):
                pe.wait_ge(dt_ready, t.idx * NG + NG)
                for g in range(NG):
                    mm = pe.matmul(ps_d[0][0:B_ROW + NS, 0:TOK], wdtn[:, g, :], dt[:, g, :],
                                   start=g == 0, stop=g == NG - 1)
                mm.then_inc(dtn_done, 1)

            def sum_states(i, st):
                g, q = st // QS, st % QS
                bank = ps_y[g % 2]
                if q == 0:
                    if i.after(1) or g > 1:
                        pe.wait_ge(y_ready, i.idx * NG + g - 1)
                    pe.wait_ge(x4_loaded[g % 2], i.idx * (8 * SEM_DMA) + (g // 2 + 1) * 4 * SEM_DMA)
                    for c in range(NC):
                        mm = pe.matmul(bank[32 * c:32 * c + 32, 0:TOK], skip_w[:, g, c, :], x4[:, g % 2, c, :],
                                       start=True, stop=False, skip_group_check=True)
                    mm.then_inc(skip_added, QS)
                pe.wait_ge(g_ready, i.idx * STEPS + st + 1)
                for c in range(NC):
                    mm = pe.matmul(bank[32 * c:32 * c + 32, 0:TOK], nsum[:], uhg[:, st % RING, c, :],
                                   start=False, stop=q == QS - 1, skip_group_check=True)
                mm.then_inc(g_used, 1)

            def y_mean(t):
                pe.wait_ge(y_ready, t.idx * NG + NG)
                pe.wait_ge(sz_ready, t.idx * NG + NG)
                if t.after(1):
                    pe.wait_ge(res_added, t.idx * KT - KT + 2)
                for g in range(NG):
                    mm = pe.matmul(ps_w[0][:, 0:TOK], mean_w[:], y[:, t.s % 2, g, :], start=g == 0, stop=g == NG - 1)
                mm.then_inc(mean_done, 1)

            def y_var(t, lo, hi):
                if lo == 0:
                    pe.wait_ge(sz_ready, t.idx * NG + 3)
                    if t.after(1):
                        pe.wait_ge(res_added, t.idx * KT - KT + 1)
                for g in range(lo, hi):
                    pe.wait_ge(squared, t.idx * NG + g + 1)
                    pe.matmul(ps_w[1][:, 0:TOK], mean_w[:], sq[:, g, :],
                              start=g == 0, stop=g == NG - 1).then_inc(sq_used, 1)

            def z_project(t, g):
                bank = ps_w[1 - g % 2]
                if g == 0:
                    pe.wait_ge(xlnT_ready, t.idx * KM + KM)
                    if t.after(1):
                        pe.wait_ge(rstd_ready, t.idx)
                elif g == 1:
                    if t.at(1).exists():
                        pe.wait_ge(xp_ready, t.idx + 2)
                    if t.after(1):
                        pe.wait_ge(centred, t.idx)
                else:
                    pe.wait_ge(sz_ready, t.idx * NG + g - 1)
                for m in range(KM):
                    mm = pe.matmul(bank[:, 0:TOK], win[:, m, DI + g * P:DI + (g + 1) * P],
                                   xlnT[:, t.s % XLN_TILES, m, :], start=m == 0, stop=m == KM - 1)
                mm.then_inc(z_done, 1)

            def out_project(t, k):
                nxt = t.at(1)
                if k == 0:
                    pe.wait_ge(gated, t.idx * NG + NG)
                    pe.wait_ge(rstd_ready, t.idx + 1)
                    if nxt.exists():
                        pe.wait_ge(sz_ready, nxt.idx * NG + 3)
                elif k == 1:
                    pe.wait_ge(centred, t.idx + 1)
                    if nxt.exists():
                        pe.wait_ge(sz_ready, nxt.idx * NG + 4)
                else:
                    if t.after(1):
                        pe.wait_ge(res_added, t.idx * KT)
                    if nxt.at(1).exists():
                        pe.wait_ge(dt_ready, nxt.idx * NG + NG + 2)
                for g in range(NG):
                    pe.matmul(ps_out[k][:, 0:DM], y[:, t.s % 2, g, k * P:(k + 1) * P], wout[:, g, :],
                              start=g == 0, stop=False)
                pe.matmul(ps_out[k][:, 0:DM], ones_row[:], bout[:], start=False, stop=True).then_inc(out_done, 1)

            def body(b):
                for s in range(TPB):
                    i = Tile(b, s)
                    prev, nxt, ahead = i.at(-1), i.at(1), i.at(3)
                    for st in range(STEPS):
                        if nxt.exists():
                            if st == 7:
                                x_project(nxt)
                            if st == 8:
                                dt_project(nxt)
                        if st == 10:
                            z_project(i, 0)
                            z_project(i, 1)
                        if prev.exists() and st == 14:
                            out_project(prev, 0)
                            out_project(prev, 1)
                        if ahead.exists() and st == 15:
                            project(ahead, 2)
                            project(ahead, 3)
                        if st >= 2:
                            sum_states(i, st - 2)
                        elif prev.exists():
                            sum_states(prev, st + STEPS - 2)
                        if nxt.exists():
                            if 1 <= st <= NG:
                                conv(nxt, st - 1, nxt.at(1) if nxt.at(1).exists() else nxt)
                            if st == 12:
                                dtn_project(nxt)
                        if ahead.exists() and st == 12:
                            transpose_x(ahead, lambda m: pe.wait_ge(dt_ready, nxt.idx * NG + 3 + m))
                        if st == 11:
                            z_project(i, 2)
                            z_project(i, 3)
                        if prev.exists():
                            if st == 2:
                                y_mean(prev)
                            if st == 5:
                                y_var(prev, 0, NG)
                            if st == 14:
                                out_project(prev, 2)
                        if ahead.exists() and st == 13:
                            project(ahead, 0)
                            project(ahead, 1)

            def start_tile(t, ps_free):
                transpose_x(t, ps_free)
                for c in range(NC):
                    project(t, c)

            pe.wait_ge(ident_set, 2)
            pe.wait_ge(win_in, SEM_DMA)
            start_tile(Tile(0, 0), lambda m: None)
            start_tile(Tile(0, 1), lambda m: pe.wait_ge(xh_ready, NC - 1 + m))
            pe.wait_ge(weights_in, WEIGHT_DMAS * SEM_DMA)
            pe.wait_ge(masks_set, 1)
            pe.wait_ge(consts_set, 1)
            pe.wait_ge(pads_set, 1)
            for g in range(NG):
                conv(Tile(0, 0), g, Tile(0, 1))
            x_project(Tile(0, 0))
            dt_project(Tile(0, 0))
            dtn_project(Tile(0, 0))
            start_tile(Tile(0, 2), lambda m: pe.wait_ge(dt_ready, 3 + m))
            body(0)
            with pe.Fori(1, IMAGES - 1) as b:
                body(b)
            body(IMAGES - 1)
            last = Tile(IMAGES - 1, TPB - 1)
            sum_states(last, STEPS - 2)
            sum_states(last, STEPS - 1)
            y_mean(last)
            y_var(last, 0, NG)
            for k in range(KT):
                out_project(last, k)

        @block.scalar
        def _(act):
            def decay(i, st):
                g, q = st // QS, st % QS
                if q == 0:
                    act.wait_ge(dt4_loaded[g % 2], i.idx * (8 * SEM_DMA) + (g // 2 + 1) * 4 * SEM_DMA)
                if i.after(1) or st > 1:
                    act.wait_ge(h_ready, i.idx * STEPS + st - 1)
                act.activation(a[:, st % 2], dt4[:, g % 2], ACT.Exp, scale=a4[:, q:q + 1]).then_inc(a_ready, 1)

            def ln1_log_var(t):
                act.wait_ge(ln1_var, t.idx + 1)
                if t.after(1):
                    act.wait_ge(xln_ready, t.idx)
                act.activation(rs1[:], mv1[:, :, 1], ACT.Ln, bias=eps1[:]).then_inc(ln1_log, 1)

            def ln1_scale(t):
                act.wait_ge(ln1_log, t.idx + 1)
                act.activation(rs1[:], rs1[:], ACT.Exp, scale=-0.5).then_inc(ln1_rstd, 1)

            def ln2_scale(t):
                act.wait_ge(ln2_var, t.idx + 1)
                if t.after(1):
                    act.wait_ge(final_ready, t.idx)
                act.activation(rs2[:], mv2[:, :, 1], ACT.Ln, bias=eps2[:]).then_inc(ln2_log, 1)
                act.wait_ge(ln2_log, t.idx + 1)
                act.activation(rs2[:], rs2[:], ACT.Exp, scale=-0.5).then_inc(ln2_rstd, 1)

            def copy_xlnT(t):
                for m in range(KM):
                    act.wait_ge(xt_done, t.idx * KM + m + 1)
                    if t.after(3) and m == 0:
                        act.wait_ge(z_done, t.idx * NG - 2 * NG)
                    act.activation(xlnT[:, t.s % XLN_TILES, m, :], ps_c[m][:, 0:TOK], ACT.Copy).then_inc(xlnT_ready, 1)

            def copy_xh(t, c):
                act.wait_ge(proj_done, t.idx * NC + c + 1)
                if t.after(3) and c == 0:
                    for n in range(2):
                        act.wait_ge(xh4_loaded[n], t.idx * (8 * SEM_DMA) - 8 * SEM_DMA)
                slot = t.s % XH_TILES
                act.activation(xh[:, c, slot * ROWS:(slot + 1) * ROWS, 1:1 + SIDE],
                               ps_c[c % 2][:, 0:TOK].rearrange("p (r w) -> p r w", r=ROWS), ACT.Copy) \
                   .then_inc(xh_ready, 1)

            def copy_xc(t, g):
                act.wait_ge(conv_done, t.idx * NG + g + 1)
                if t.after(2) and g == 0:
                    for n in range(2):
                        act.wait_ge(x4_loaded[n], t.idx * (8 * SEM_DMA) - 8 * SEM_DMA)
                act.activation(xc[:, t.s % 2, g, :], ps_c[g % 2][:, 0:TOK], ACT.Copy).then_inc(xc_ready, 1)

            def copy_xp(t):
                act.wait_ge(xproj_done, t.idx + 1)
                if t.after(1):
                    act.wait_ge(dtp_done, t.idx * NC)
                    act.wait_ge(db_ready, t.idx)
                    act.wait_ge(bounced, t.idx * (2 * SEM_DMA))
                act.activation(xp[:], ps_w[0][0:XP_ROWS, 0:TOK], ACT.Identity, bias=xp_one[:]).then_inc(xp_ready, 1)

            def softplus_abs(t, g):
                act.wait_ge(dtp_done, t.idx * NG + g + 1)
                if t.after(1) and g == 0:
                    for n in range(2):
                        act.wait_ge(dt4_loaded[n], t.idx * (8 * SEM_DMA))
                    act.wait_ge(dtn_done, t.idx)
                act.activation(dt[:, g, :], ps_dt[g][:, 0:TOK], ACT.Abs).then_inc(sp_abs, 1)

            def softplus_exp(t, g):
                act.wait_ge(sp_abs, t.idx * NG + g + 1)
                act.activation(dt[:, g, :], dt[:, g, :], ACT.Exp, scale=-1.0).then_inc(sp_exp, 1)

            def softplus_log(t, g):
                act.wait_ge(sp_exp, t.idx * NG + g + 1)
                act.activation(dt[:, g, :], dt[:, g, :], ACT.Ln, bias=one_c[:]).then_inc(sp_log, 1)

            def copy_y(i, g):
                act.wait_ge(g_used, i.idx * STEPS + QS * (g + 1))
                if i.after(2) and g == 0:
                    act.wait_ge(out_done, i.idx * KT - KT)
                act.activation(y[:, i.s % 2, g, :], ps_y[g % 2][:, 0:TOK], ACT.Copy).then_inc(y_ready, 1)

            def square(t, g):
                if g == 0:
                    act.wait_ge(centred, t.idx + 1)
                    if t.after(1):
                        act.wait_ge(sq_used, t.idx * NG)
                act.activation(sq[:, g, :], y[:, t.s % 2, g, :], ACT.Square).then_inc(squared, 1)

            def y_log_var(t):
                act.wait_ge(sq_used, t.idx * NG + NG)
                if t.after(1):
                    act.wait_ge(normed, t.idx * NG)
                act.activation(rstd[:], ps_w[1][:, 0:TOK], ACT.Ln, bias=eps2[:]).then_inc(var_log, 1)

            def y_scale(t):
                act.wait_ge(var_log, t.idx + 1)
                act.activation(rstd[:], rstd[:], ACT.Exp, scale=-0.5).then_inc(rstd_ready, 1)

            def gate(t, g):
                if t.after(1) and g == 0:
                    act.wait_ge(gated, t.idx * NG)
                act.wait_ge(z_done, t.idx * NG + g + 1)
                act.activation(sz[:, g, :], ps_w[1 - g % 2][:, 0:TOK], ACT.Silu).then_inc(sz_ready, 1)

            def body(b):
                for s in range(TPB):
                    i = Tile(b, s)
                    prev, nxt, ahead = i.at(-1), i.at(1), i.at(3)
                    for st in range(STEPS):
                        decay(i, st)
                        if st < 2 and i.after(1) and i.at(2).exists():
                            copy_xh(i.at(2), 2 * st)
                            copy_xh(i.at(2), 2 * st + 1)
                        if nxt.exists():
                            if 3 <= st < 3 + NG:
                                copy_xc(nxt, st - 3)
                            if st == 8:
                                copy_xp(nxt)
                        if prev.exists():
                            if st == 1 and i.after(2):
                                ln2_scale(i.at(-2))
                            if st == 2:
                                copy_y(prev, 3)
                            if st == 5:
                                for g in range(NG):
                                    square(prev, g)
                            if st == 7:
                                y_log_var(prev)
                                y_scale(prev)
                        if st in (6, 10, 14):
                            copy_y(i, (st - 6) // 4)
                        if st == 9 and nxt.exists():
                            for g in range(NG):
                                softplus_abs(nxt, g)
                            for g in range(NG):
                                softplus_exp(nxt, g)
                        if st == 10:
                            if nxt.exists():
                                for g in range(NG):
                                    softplus_log(nxt, g)
                            if ahead.exists():
                                ln1_log_var(ahead)
                                ln1_scale(ahead)
                        if st == 11:
                            gate(i, 0)
                            gate(i, 1)
                        if st == 12:
                            gate(i, 2)
                            gate(i, 3)
                        if ahead.exists():
                            if st == 13:
                                copy_xlnT(ahead)

            def ln1(t):
                ln1_log_var(t)
                ln1_scale(t)

            def copy_tile(t):
                copy_xlnT(t)
                for c in range(NC):
                    copy_xh(t, c)

            act.wait_ge(consts_set, 1)
            ln1(Tile(0, 0))
            act.wait_ge(pads_set, 1)
            copy_tile(Tile(0, 0))
            ln1(Tile(0, 1))
            copy_tile(Tile(0, 1))
            act.wait_ge(weights_in, WEIGHT_DMAS * SEM_DMA)
            act.activation(a4[:], a4[:], ACT.Exp).then_inc(a_exp, 1)
            t = Tile(0, 0)
            for g in range(NG):
                copy_xc(t, g)
            act.wait_ge(nsum_set, 7)
            copy_xp(t)
            for g in range(NG):
                softplus_abs(t, g)
            for g in range(NG):
                softplus_exp(t, g)
            for g in range(NG):
                softplus_log(t, g)
            ln1(Tile(0, 2))
            copy_tile(Tile(0, 2))
            act.wait_ge(masks_set, 2)
            body(0)
            with act.Fori(1, IMAGES - 1) as b:
                body(b)
            body(IMAGES - 1)
            last = Tile(IMAGES - 1, TPB - 1)
            ln2_scale(last.at(-1))
            copy_y(last, 3)
            for g in range(NG):
                square(last, g)
            y_log_var(last)
            y_scale(last)
            ln2_scale(last)

        FFN = 14

        @block.vector
        def _(dve):
            def step_input(i, st):
                g, q = st // QS, st % QS
                if q == 0:
                    dve.wait_ge(x4_loaded[g % 2], i.idx * (8 * SEM_DMA) + (g // 2 + 1) * 4 * SEM_DMA)
                if st == 0:
                    dve.wait_ge(db4_loaded[i.s % 2], i.half * (4 * SEM_DMA) + 4 * SEM_DMA)
                if i.after(1) or st >= RING:
                    dve.wait_ge(g_used, i.idx * STEPS + st - RING + 1)
                dve.tensor_tensor(uhg[:, st % RING], x4[:, g % 2],
                                  db4[:, i.s % 2, q:q + 1, :].broadcast_to([P, NC, TOK]), ALU.mult) \
                   .then_inc(u_ready, 2 if q == POOL_Q - 1 else 1)

            def recur(i, st):
                g, q = st // QS, st % QS
                if q == POOL_Q:
                    dve.wait_ge(pool_u_ready, i.idx * STEPS + QS * (g + 1))
                else:
                    dve.wait_ge(u_ready, i.idx * STEPS + st + (2 if q == POOL_Q - 1 else 1))
                dve.wait_ge(a_ready, i.idx * STEPS + st + 1)
                if not i.first_of_image():
                    dve.wait_ge(carry_saved, carries(i.at(-1), st))
                for c in range(NC):
                    h0 = 0.0 if i.first_of_image() else carry[:, st, c:c + 1]
                    ins = dve.tensor_tensor_scan(uhg[:, st % RING, c, :], a[:, st % 2, c, :], uhg[:, st % RING, c, :],
                                                 h0, ALU.mult, ALU.add)
                ins.then_inc(h_ready, 1)

            def ln1_stats(t):
                dve.wait_ge(xin_loaded, t.idx * SEM_DMA + SEM_DMA)
                for k in range(KT):
                    ins = dve.bn_stats(st1[:, k, :], xin[:, k, :])
                ins.then_inc(ln1_stat, 1)

            def ln1_aggregate(t):
                dve.wait_ge(ln1_stat, t.idx + 1)
                dve.memset(wait_pad1[:], 0.0)
                for k in range(KT):
                    ins = dve.bn_aggr(mv1[:, k, :], st1[:, k, :])
                ins.then_inc(ln1_var, 1)

            def ln1_apply(t):
                dve.wait_ge(ln1_var, t.idx + 1)
                dve.wait_ge(ln1_rstd, t.idx + 1)
                for k in range(KT):
                    ins = dve.tensor_scalar(xin[:, k, :], xin[:, k, :], mv1[:, k, 0:1], rs1[:, k:k + 1],
                                            ALU.subtract, ALU.mult)
                ins.then_inc(xln_ready, 1)

            def finish_dt(t, g):
                dve.wait_ge(sp_log, t.idx * NG + g + 1)
                dve.scalar_tensor_tensor(dt[:, g, :], ps_dt[g][:, 0:TOK], 0.0, dt[:, g, :],
                                         ALU.max, ALU.add).then_inc(dt_ready, 1)

            def make_db(t):
                dve.wait_ge(dtn_done, t.idx + 1)
                dve.wait_ge(xp_ready, t.idx + 1)
                if t.after(1):
                    dve.wait_ge(bounced, t.idx * (2 * SEM_DMA))
                rows = slice(B_ROW, B_ROW + NS)
                dve.scalar_tensor_tensor(dbt[rows, :], ps_d[0][rows, 0:TOK], bdtn[rows, :], xp[rows, :],
                                         ALU.add, ALU.mult).then_inc(db_ready, 1)

            def centre(t):
                dve.wait_ge(mean_done, t.idx + 1)
                ys = y[:, t.s % 2]
                mean = ps_w[0][:, 0:TOK].unsqueeze(1).broadcast_to([P, NG, TOK])
                dve.tensor_tensor(ys, ys, mean, ALU.subtract).then_inc(centred, 1)

            def norm(t, g):
                if g == 0:
                    dve.wait_ge(rstd_ready, t.idx + 1)
                    dve.wait_ge(centred, t.idx + 1)
                ys = y[:, t.s % 2, g, :]
                dve.scalar_tensor_tensor(ys, ys, gam[:, g:g + 1], rstd[:], ALU.mult, ALU.mult).then_inc(normed, 1)

            def gate_y(t, g):
                dve.wait_ge(normed, t.idx * NG + g + 1)
                dve.wait_ge(sz_ready, t.idx * NG + g + 1)
                ys = y[:, t.s % 2, g, :]
                dve.scalar_tensor_tensor(ys, ys, bet[:, g:g + 1], sz[:, g, :], ALU.add, ALU.mult).then_inc(gated, 1)

            def add_residual(t, k):
                if k == 0:
                    dve.wait_ge(res_loaded, t.idx * SEM_DMA + SEM_DMA)
                dve.wait_ge(out_done, t.idx * KT + k + 1)
                dve.tensor_tensor(res[:, k, :], res[:, k, :], ps_out[k][:, 0:DM], ALU.add).then_inc(res_added, 1)

            def ln2_stats(t):
                dve.wait_ge(res_added, t.idx * KT + KT)
                for k in range(KT):
                    ins = dve.bn_stats(st2[:, k, :], res[:, k, :])
                ins.then_inc(ln2_stat, 1)

            def ln2_aggregate(t):
                dve.wait_ge(ln2_stat, t.idx + 1)
                dve.memset(wait_pad2[:], 0.0)
                for k in range(KT):
                    ins = dve.bn_aggr(mv2[:, k, :], st2[:, k, :])
                ins.then_inc(ln2_var, 1)

            def ffn_stage(t, n):
                if n == 0:
                    dve.wait_ge(ln2_rstd, t.idx + 1)
                    dve.wait_ge(ln2_var, t.idx + 1)
                else:
                    dve.wait_ge(ffn, t.idx * FFN + n)
                if n == 0:
                    for k in range(KT):
                        dve.tensor_scalar(hot[:, k, :], res[:, k, 0:64], mv2[:, k, 0:1], rs2[:, k:k + 1],
                                          ALU.subtract, ALU.mult)
                    dve.tensor_scalar(sc1[:], rs2[:], 1.0, None, ALU.add)
                    ins = dve.tensor_tensor(sc2[:], rs2[:], mv2[:, :, 0], ALU.mult)
                elif n == 1:
                    for k in range(KT):
                        dve.tensor_scalar(res[:, k, :], res[:, k, :], sc1[:, k:k + 1], sc2[:, k:k + 1],
                                          ALU.mult, ALU.subtract)
                    ins = dve.tensor_scalar(hot[:], hot[:], 0.5, None, ALU.is_gt)
                elif n == 2:
                    for w in range(3):
                        dve.tensor_tensor(score[:, :, w, :], hot[:, :, 32 + 8 * w:48 + 8 * w],
                                          score16[:].unsqueeze(1).broadcast_to([P, KT, 16]), ALU.mult)
                    ins = dve.tensor_tensor(amp[:], hot[:, :, 39], hot[:, :, 40], ALU.max)
                elif n == 3:
                    dve.scalar_tensor_tensor(amp[:], amp[:], 2.0, hot[:, :, 0], ALU.mult, ALU.mult)
                    ins = dve.tensor_reduce(best[:], score[:], AX_X, ALU.max)
                elif n == 4:
                    ins = dve.tensor_scalar(found[:], best[:], 0.0, None, ALU.is_gt)
                elif n == 5:
                    ins = dve.tensor_scalar(best[:], best[:], -1.0, 16.0, ALU.mult, ALU.add)
                elif n == 6:
                    ins = dve.tensor_tensor(nib[:], best[:], found[:], ALU.mult)
                elif n == 7:
                    ins = dve.scalar_tensor_tensor(val[:], nib[:, :, 1], 16.0, nib[:, :, 0], ALU.mult, ALU.add)
                elif n == 8:
                    dve.tensor_tensor(shl[:], val[:], nib[:, :, 2], ALU.logical_shift_left)
                    ins = dve.tensor_tensor(shr[:], val[:], nib[:, :, 2], ALU.logical_shift_right)
                elif n == 9:
                    ins = dve.tensor_single_scalar(shl[:], shl[:], 255, ALU.bitwise_and)
                elif n == 10:
                    ins = dve.tensor_tensor(dif[:], shl[:], shr[:], ALU.subtract)
                elif n == 11:
                    ins = dve.tensor_tensor(dif[:], dif[:], hot[:, :, 39], ALU.mult)
                elif n == 12:
                    ins = dve.tensor_tensor(resi[:], dif[:], shr[:], ALU.add)
                elif n == 13:
                    dve.tensor_single_scalar(rnib[:, :, 0], resi[:], 15, ALU.bitwise_and)
                    ins = dve.tensor_single_scalar(rnib[:, :, 1], resi[:], 4, ALU.logical_shift_right)
                ins.then_inc(ffn, 1)

            def ffn_mark(t):
                dve.wait_ge(ffn, t.idx * FFN + FFN)
                for w in range(2):
                    ins = dve.tensor_tensor(hots[:, :, w, :], rnib[:, :, w:w + 1].broadcast_to([P, KT, 16]),
                                            idx16[:].unsqueeze(1).broadcast_to([P, KT, 16]), ALU.is_equal)
                ins.then_inc(marked, 1)

            def ffn_weigh(t):
                dve.wait_ge(marked, t.idx * 3 + 1)
                for w in range(2):
                    ins = dve.tensor_tensor(hots[:, :, w, :], hots[:, :, w, :],
                                            amp[:].unsqueeze(2).broadcast_to([P, KT, 16]), ALU.mult)
                ins.then_inc(marked, 1)

            def ffn_add_low(t):
                dve.wait_ge(marked, t.idx * 3 + 2)
                dve.tensor_tensor(res[:, :, 64:80], res[:, :, 64:80], hots[:, :, 0, :], ALU.add).then_inc(marked, 1)

            def ffn_add_high(t):
                dve.wait_ge(marked, t.idx * 3 + 3)
                dve.tensor_tensor(res[:, :, 72:88], res[:, :, 72:88], hots[:, :, 1, :], ALU.add) \
                   .then_inc(final_ready, 1)

            def body(b):
                for s in range(TPB):
                    i = Tile(b, s)
                    before, prev, nxt, ahead = i.at(-2), i.at(-1), i.at(1), i.at(3)
                    for st in range(STEPS):
                        if st + 1 < STEPS and (st + 1) % QS != POOL_Q:
                            step_input(i, st + 1)
                        if before.exists():
                            if 2 <= st < 9:
                                ffn_stage(before, 2 * st - 4)
                            if st == 9:
                                ffn_mark(before)
                            if st == 10:
                                ffn_add_low(before)
                        if prev.exists():
                            if st == 4:
                                centre(prev)
                            if st == 8:
                                for g in range(NG):
                                    norm(prev, g)
                            if st == 10:
                                for g in range(NG):
                                    gate_y(prev, g)
                        if nxt.exists():
                            if st == 11:
                                for g in range(NG):
                                    finish_dt(nxt, g)
                            if st == 13:
                                make_db(nxt)
                        if ahead.exists():
                            if st == 6:
                                ln1_stats(ahead)
                            if st == 7:
                                ln1_aggregate(ahead)
                        recur(i, st)
                        if before.exists():
                            if 2 <= st < 9:
                                ffn_stage(before, 2 * st - 3)
                            if st == 9:
                                ffn_weigh(before)
                            if st == 10:
                                ffn_add_high(before)
                        if ahead.exists() and st == 10:
                            ln1_apply(ahead)
                    if nxt.exists():
                        step_input(nxt, 0)
                    if prev.exists():
                        for k in range(KT):
                            add_residual(prev, k)
                        ln2_stats(prev)
                        ln2_aggregate(prev)

            def finish(t):
                for n in range(FFN):
                    ffn_stage(t, n)
                ffn_mark(t)
                ffn_weigh(t)
                ffn_add_low(t)
                ffn_add_high(t)

            dve.memset(wxp[:], 0.0).then_inc(zeros_set, 1)
            dve.memset(wdtn[:], 0.0).then_inc(zeros_set, 1)
            dve.memset(zero_row[:], 0.0)
            dve.memset(taps[96:P], 0.0).then_inc(zeros_set, 1)
            dve.memset(xh4[96:P], 0.0)
            dve.memset(xh[:, :, :, 0:1], 0.0)
            dve.memset(xh[:, :, :, SIDE + 1:SIDE + 2], 0.0).then_inc(pads_set, 1)
            dve.memset(mean_w[:], 1.0 / DI)
            dve.memset(ones_row[:], 1.0)
            dve.memset(one_c[:], 1.0)
            dve.memset(eps1[:], 1e-6)
            dve.memset(eps2[:], 1e-5).then_inc(consts_set, 1)
            for s in range(2):
                ln1_stats(Tile(0, s))
                ln1_aggregate(Tile(0, s))
                ln1_apply(Tile(0, s))
            dve.wait_ge(nsum_set, 5)
            dve.wait_ge(weights_in, WEIGHT_DMAS * SEM_DMA)
            dve.wait_ge(zeros_set, 3)
            for x in range(3):
                dve.tensor_tensor(conv_w[:, x], nsum[:].unsqueeze(1).broadcast_to([P, BLOCKS, 32]),
                                  taps[:, x].unsqueeze(2).broadcast_to([P, BLOCKS, 32]), ALU.mult)
            for g in range(NG):
                for c in range(NC):
                    ins = dve.tensor_scalar(skip_w[:, g, c, :], nsum[:], dskip4[:, g, c:c + 1], 0.25,
                                            ALU.mult, ALU.mult)
            ins.then_inc(masks_set, 1)
            dve.wait_ge(a_exp, 1)
            dve.tensor_scalar(a4[:], a4[:], -1.0, None, ALU.mult).then_inc(masks_set, 1)
            dve.wait_ge(idx_set, 2)
            ln1_stats(Tile(0, 2))
            ln1_aggregate(Tile(0, 2))
            t = Tile(0, 0)
            for g in range(NG):
                finish_dt(t, g)
            ln1_apply(Tile(0, 2))
            make_db(t)
            step_input(t, 0)
            body(0)
            with dve.Fori(1, IMAGES - 1) as b:
                body(b)
            body(IMAGES - 1)
            last = Tile(IMAGES - 1, TPB - 1)
            finish(last.at(-1))
            centre(last)
            for g in range(NG):
                norm(last, g)
            for g in range(NG):
                gate_y(last, g)
            for k in range(KT):
                add_residual(last, k)
            ln2_stats(last)
            ln2_aggregate(last)
            finish(last)

        @block.gpsimd
        def _(pool):
            def pool_input(i, g):
                st = QS * g + POOL_Q
                pool.wait_ge(x4_loaded[g % 2], i.idx * (8 * SEM_DMA) + (g // 2 + 1) * 4 * SEM_DMA)
                pool.wait_ge(db4_loaded[i.s % 2], i.half * (4 * SEM_DMA) + 4 * SEM_DMA)
                if i.after(1) or st >= RING:
                    pool.wait_ge(g_used, i.idx * STEPS + st - RING + 1)
                pool.tensor_tensor(uhg[:, st % RING], x4[:, g % 2],
                                   db4[:, i.s % 2, POOL_Q:POOL_Q + 1, :].broadcast_to([P, NC, TOK]), ALU.mult) \
                    .then_inc(pool_u_ready, QS)

            def save_carry(i, st):
                pool.wait_ge(h_ready, i.idx * STEPS + st + 1)
                pool.tensor_tensor(carry[:, st, :], uhg[:, st % RING, :, TOK - 1], one_nc[:], ALU.mult) \
                    .then_inc(carry_saved, 1)

            def weigh(i, st):
                q = st % QS
                pool.wait_ge(h_ready, i.idx * STEPS + st + 1)
                if not i.last_of_image():
                    pool.wait_ge(carry_saved, carries(i, st))
                if st == 0:
                    pool.wait_ge(c4_loaded[i.s % 2], i.half * (4 * SEM_DMA) + 4 * SEM_DMA)
                slot = uhg[:, st % RING]
                pool.tensor_tensor(slot, slot, c4[:, i.s % 2, q:q + 1, :].broadcast_to([P, NC, TOK]), ALU.mult) \
                    .then_inc(g_ready, 1)

            def body(b):
                for s in range(TPB):
                    i = Tile(b, s)
                    for st in range(STEPS):
                        if st % QS == POOL_Q - 2:
                            pool_input(i, st // QS)
                        if not i.last_of_image():
                            save_carry(i, st)
                        weigh(i, st)

            pool.memset(one_nc[:], 1.0)
            pool.memset(ident[:], 0.0).then_inc(ident_set, 1)
            pool.wait_ge(ident_set, 1)
            pool.affine_select(out=ident[:], in_=ident[:], compare_op=ALU.not_equal, fill=1.0, base=0,
                               pattern=[[-1, P]], channel_multiplier=1).then_inc(ident_set, 1)
            pool.memset(nsum[:], 0.0).then_inc(nsum_set, 1)
            for k in range(4):
                pool.wait_ge(nsum_set, k + 1)
                pool.affine_select(out=nsum[:], in_=nsum[:], compare_op=ALU.not_equal, fill=1.0, base=-32 * k,
                                   pattern=[[-1, 32]], channel_multiplier=1).then_inc(nsum_set, 1)
            pool.memset(xp_one[:], 0.0).then_inc(nsum_set, 1)
            pool.wait_ge(nsum_set, 6)
            pool.affine_select(out=xp_one[:], in_=xp_one[:], compare_op=ALU.not_equal, fill=1.0, base=-DTR,
                               pattern=[[0, 1]], channel_multiplier=1).then_inc(nsum_set, 1)
            pool.iota(idx16[:], pattern=[[1, 16]], base=0, channel_multiplier=0,
                      allow_small_or_imprecise_dtypes=True).then_inc(idx_set, 1)
            pool.iota(score16[:], pattern=[[-1, 16]], base=16, channel_multiplier=0,
                      allow_small_or_imprecise_dtypes=True).then_inc(idx_set, 1)
            body(0)
            with pool.Fori(1, IMAGES - 1) as b:
                body(b)
            body(IMAGES - 1)


_INS = ['x', 'L0_conv_W_in', 'L0_conv_conv_k', 'L0_conv_W_xproj', 'L0_conv_W_dt', 'L0_conv_b_dt', 'L0_conv_A_log',
        'L0_conv_Dskip', 'L0_conv_W_dtN', 'L0_conv_b_dtN', 'L0_conv_ln_g', 'L0_conv_ln_b', 'L0_conv_W_out',
        'L0_conv_b_out']
_OUTS = [((IMAGES, SIDE, SIDE, DM), 'float32')]


def kernel(**inputs):
    import numpy as _np
    import concourse.bacc as _bacc
    from concourse import mybir as _mybir
    from concourse.bass_utils import run_bass_kernel_spmd as _run

    nc = _bacc.Bacc("TRN2", target_bir_lowering=False, num_devices=1)
    arrays, args = {}, []
    for name in _INS:
        a = _np.ascontiguousarray(inputs[name])
        arrays[f"in_{name}_dram"] = a
        args.append(nc.dram_tensor(f"in_{name}_dram", a.shape, _mybir.dt.from_np(a.dtype), kind="ExternalInput").ap())
    for i, (shape, dtype) in enumerate(_OUTS):
        dt = _mybir.dt.from_np(_np.dtype(dtype))
        args.append(nc.dram_tensor(f"out_{i}_dram", shape, dt, kind="ExternalOutput").ap())
    build(nc, *args)
    r = _run(nc, [arrays], core_ids=[0])
    got = tuple(r.results[0][f"out_{i}_dram"] for i in range(len(_OUTS)))
    return got[0]
```
